# Optimizing a Trainium2 kernel written in Bass

```python
import numpy as np
import jax
import jax.numpy as jnp

def _softmax(x, axis=-1):
    return jax.nn.softmax(x, axis=axis)

def _gelu(x):
    return jax.nn.gelu(x, approximate=True)

def _silu(x):
    return jax.nn.silu(x)

def _sigmoid(x):
    return jax.nn.sigmoid(x)

def _layernorm(x, axis=-1, eps=1e-05):
    m = jnp.mean(x, axis=axis, keepdims=True)
    v = jnp.var(x, axis=axis, keepdims=True)
    return (x - m) / jnp.sqrt(v + eps)

def _scatter_add(tgt, idx, src, axis=0):
    return tgt.at[idx].add(src)

def _segment_sum(src, seg, n):
    return jax.ops.segment_sum(src, seg, n)
kernel_name = 'mk_pixart_resid_d1_seqx_r4_e6dc56'

def setup_inputs(seed: int=0):
    np.random.seed(seed)
    _w = jnp.asarray

    def _rec_inputs():
        import jax
        import jax.numpy as jnp
        _rk = jax.random.key(seed)
        x = -0.0002928 + 1 * jax.random.normal(jax.random.fold_in(_rk, 1), (4, 512, 256), jnp.float32)
        _lenS = 512 - jax.random.randint(jax.random.fold_in(_rk, 7), (4,), 0, max(1, 512 // 4) + 1, jnp.int32)
        _lenS2 = 512 - jax.random.randint(jax.random.fold_in(_rk, 8), (4,), 0, max(1, 512 // 4) + 1, jnp.int32)
        cond_1024 = 0.0061147 + 1.02565 * jax.random.normal(jax.random.fold_in(_rk, 11), (4, 256), jnp.float32)
        _ctx_1024P = jax.random.normal(jax.random.fold_in(_rk, 12), (4, 16, 256), jnp.float32)
        _ctx_1024c = jax.random.dirichlet(jax.random.fold_in(_rk, 512), 0.3 * jnp.ones((16,), jnp.float32), (4, 512))
        _ctx_1024t = jnp.einsum('bsk,bkd->bsd', _ctx_1024c, _ctx_1024P)
        _ctx_1024t = _ctx_1024t * jax.lax.rsqrt(jnp.mean(jnp.square(_ctx_1024t)) + 1e-12) * 0.953939
        ctx_1024 = 0.00086875 + 0.999764 * (_ctx_1024t + 0.3 * jax.random.normal(jax.random.fold_in(_rk, 612), (4, 512, 256), jnp.float32))
        _validS = jnp.arange(512)[None, :] < _lenS[:, None]
        _validS2 = jnp.arange(512)[None, :] < _lenS2[:, None]
        _causal = jnp.tril(jnp.ones((512, 512), dtype=bool))
        mask_BxS_bf0 = jnp.logical_not(jnp.ones((4, 512), dtype=bool))
        mask_BxS2_bf0 = jnp.logical_not(jnp.ones((4, 512), dtype=bool))
        return (x, cond_1024, ctx_1024, mask_BxS_bf0, mask_BxS2_bf0)
    x, cond_1024, ctx_1024, mask_BxS_bf0, mask_BxS2_bf0 = _rec_inputs()

    def _L0_xcond_setup():
        import jax, jax.numpy as jnp
        import numpy as np
        NL, D, H, DFF = (6, 256, 16, 1024)
        HD = D // H

        def _rope(x):
            L = x.shape[1]
            half = HD // 2
            inv = 1.0 / 10000.0 ** (jnp.arange(half, dtype=jnp.float32) / half)
            ang = jnp.arange(L, dtype=jnp.float32)[:, None] * inv
            cos = jnp.cos(ang)[None, :, None, :]
            sin = jnp.sin(ang)[None, :, None, :]
            x1, x2 = (x[..., :half], x[..., half:])
            return jnp.concatenate([x1 * cos - x2 * sin, x1 * sin + x2 * cos], axis=-1)

        def _ln(x, eps=1e-05):
            m = jnp.mean(x, axis=-1, keepdims=True)
            v = jnp.var(x, axis=-1, keepdims=True)
            return (x - m) * jax.lax.rsqrt(v + eps)

        def _adaln(x, emb, w, b):
            gb = emb[:, 0, :] @ w.T + b
            g, be = jnp.split(gb, 2, axis=-1)
            return _ln(x) * (1.0 + g[:, None, :]) + be[:, None, :]

        def _attn(q, k, v, mask):
            scores = jnp.einsum('bqhd,bkhd->bhqk', q, k) / np.float32(np.sqrt(HD))
            scores = jnp.where(mask[:, None, None, :], jnp.float32(-jnp.inf), scores)
            w = jax.nn.softmax(scores, axis=-1)
            return jnp.einsum('bhqk,bkhd->bqhd', w, v)
        key = jax.random.key(seed)
        ks = jax.random.split(key, 20)
        B, L, LC = (4, 256, 128)
        s = 0.02
        inp = {'x': jax.random.normal(ks[0], (B, L, D), jnp.float32), 'noise_emb': jax.random.normal(ks[1], (B, 1, D), jnp.float32), 'context': jax.random.normal(ks[2], (B, LC, D), jnp.float32), 'src_mask': jnp.zeros((B, L), bool), 'ctx_mask': jnp.zeros((B, LC), bool), 'n1_w': jax.random.normal(ks[3], (NL, 2 * D, D), jnp.float32) * s, 'n1_b': jnp.zeros((NL, 2 * D), jnp.float32), 'n2_w': jax.random.normal(ks[4], (NL, 2 * D, D), jnp.float32) * s, 'n2_b': jnp.zeros((NL, 2 * D), jnp.float32), 'n3_w': jax.random.normal(ks[5], (NL, 2 * D, D), jnp.float32) * s, 'n3_b': jnp.zeros((NL, 2 * D), jnp.float32), 'qkv_w': jax.random.normal(ks[6], (NL, 3 * D, D), jnp.float32) * s, 'so_w': jax.random.normal(ks[7], (NL, D, D), jnp.float32) * s, 'cq_w': jax.random.normal(ks[8], (NL, D, D), jnp.float32) * s, 'ck_w': jax.random.normal(ks[9], (NL, D, D), jnp.float32) * s, 'cv_w': jax.random.normal(ks[10], (NL, D, D), jnp.float32) * s, 'co_w': jax.random.normal(ks[11], (NL, D, D), jnp.float32) * s, 'f1_w': jax.random.normal(ks[12], (NL, DFF, D), jnp.float32) * s, 'f1_b': jnp.zeros((NL, DFF), jnp.float32), 'f2_w': jax.random.normal(ks[13], (NL, D, DFF), jnp.float32) * s, 'f2_b': jnp.zeros((NL, D), jnp.float32)}
        return inp
    _L0_xcond_all = _L0_xcond_setup()
    _L0_xcond_in = {k: v for k, v in _L0_xcond_all.items() if k in ('n1_w', 'n1_b', 'n2_w', 'n2_b', 'n3_w', 'n3_b', 'qkv_w', 'so_w', 'cq_w', 'ck_w', 'cv_w', 'co_w', 'f1_w', 'f1_b', 'f2_w', 'f2_b')}
    del _L0_xcond_all

    def _L0_ffn_setup():
        import math
        import jax, jax.numpy as jnp
        import numpy as np
        E = 8
        K = 2
        CF = 1.25
        D = 256
        F = 512
        B, S = (4, 512)
        key = jax.random.key(seed)
        ks = jax.random.split(key, 8)
        sd = 1.0 / math.sqrt(D)
        sf = 1.0 / math.sqrt(F)
        return {'x': jax.random.normal(ks[0], (B, S, D), jnp.float32), 'router_w': jax.random.normal(ks[1], (D, E), jnp.float32) * sd, 'router_b': jnp.zeros((E,), jnp.float32), 'w1': jax.random.normal(ks[2], (E, D, F), jnp.float32) * sd, 'b1': jax.random.normal(ks[3], (E, F), jnp.float32) * 0.01, 'w2': jax.random.normal(ks[4], (E, F, D), jnp.float32) * sf, 'b2': jax.random.normal(ks[5], (E, D), jnp.float32) * 0.01}
    _L0_ffn_all = _L0_ffn_setup()
    _L0_ffn_in = {k: v for k, v in _L0_ffn_all.items() if k in ('router_w', 'router_b', 'w1', 'b1', 'w2', 'b2')}
    del _L0_ffn_all
    return {'x': x, 'cond_1024': cond_1024, 'ctx_1024': ctx_1024, 'mask_BxS_bf0': mask_BxS_bf0, 'mask_BxS2_bf0': mask_BxS2_bf0, 'L0_xcond_n1_w': _L0_xcond_in['n1_w'], 'L0_xcond_n1_b': _L0_xcond_in['n1_b'], 'L0_xcond_n2_w': _L0_xcond_in['n2_w'], 'L0_xcond_n2_b': _L0_xcond_in['n2_b'], 'L0_xcond_n3_w': _L0_xcond_in['n3_w'], 'L0_xcond_n3_b': _L0_xcond_in['n3_b'], 'L0_xcond_qkv_w': _L0_xcond_in['qkv_w'], 'L0_xcond_so_w': _L0_xcond_in['so_w'], 'L0_xcond_cq_w': _L0_xcond_in['cq_w'], 'L0_xcond_ck_w': _L0_xcond_in['ck_w'], 'L0_xcond_cv_w': _L0_xcond_in['cv_w'], 'L0_xcond_co_w': _L0_xcond_in['co_w'], 'L0_xcond_f1_w': _L0_xcond_in['f1_w'], 'L0_xcond_f1_b': _L0_xcond_in['f1_b'], 'L0_xcond_f2_w': _L0_xcond_in['f2_w'], 'L0_xcond_f2_b': _L0_xcond_in['f2_b'], 'L0_ffn_router_w': _L0_ffn_in['router_w'], 'L0_ffn_router_b': _L0_ffn_in['router_b'], 'L0_ffn_w1': _L0_ffn_in['w1'], 'L0_ffn_b1': _L0_ffn_in['b1'], 'L0_ffn_w2': _L0_ffn_in['w2'], 'L0_ffn_b2': _L0_ffn_in['b2']}

def reference(x, cond_1024, ctx_1024, mask_BxS_bf0, mask_BxS2_bf0, L0_xcond_n1_w, L0_xcond_n1_b, L0_xcond_n2_w, L0_xcond_n2_b, L0_xcond_n3_w, L0_xcond_n3_b, L0_xcond_qkv_w, L0_xcond_so_w, L0_xcond_cq_w, L0_xcond_ck_w, L0_xcond_cv_w, L0_xcond_co_w, L0_xcond_f1_w, L0_xcond_f1_b, L0_xcond_f2_w, L0_xcond_f2_b, L0_ffn_router_w, L0_ffn_router_b, L0_ffn_w1, L0_ffn_b1, L0_ffn_w2, L0_ffn_b2):
    import jax
    import jax.numpy as jnp

    def _L0_xcond_ref(x, noise_emb, context, src_mask, ctx_mask, n1_w, n1_b, n2_w, n2_b, n3_w, n3_b, qkv_w, so_w, cq_w, ck_w, cv_w, co_w, f1_w, f1_b, f2_w, f2_b):
        import jax, jax.numpy as jnp
        import numpy as np
        NL, D, H, DFF = (6, 256, 16, 1024)
        HD = D // H

        def _rope(x):
            L = x.shape[1]
            half = HD // 2
            inv = 1.0 / 10000.0 ** (jnp.arange(half, dtype=jnp.float32) / half)
            ang = jnp.arange(L, dtype=jnp.float32)[:, None] * inv
            cos = jnp.cos(ang)[None, :, None, :]
            sin = jnp.sin(ang)[None, :, None, :]
            x1, x2 = (x[..., :half], x[..., half:])
            return jnp.concatenate([x1 * cos - x2 * sin, x1 * sin + x2 * cos], axis=-1)

        def _ln(x, eps=1e-05):
            m = jnp.mean(x, axis=-1, keepdims=True)
            v = jnp.var(x, axis=-1, keepdims=True)
            return (x - m) * jax.lax.rsqrt(v + eps)

        def _adaln(x, emb, w, b):
            gb = emb[:, 0, :] @ w.T + b
            g, be = jnp.split(gb, 2, axis=-1)
            return _ln(x) * (1.0 + g[:, None, :]) + be[:, None, :]

        def _attn(q, k, v, mask):
            scores = jnp.einsum('bqhd,bkhd->bhqk', q, k) / np.float32(np.sqrt(HD))
            scores = jnp.where(mask[:, None, None, :], jnp.float32(-jnp.inf), scores)
            w = jax.nn.softmax(scores, axis=-1)
            return jnp.einsum('bhqk,bkhd->bqhd', w, v)
        B, L, _ = x.shape
        LC = context.shape[1]
        for i in range(NL):
            xn = _adaln(x, noise_emb, n1_w[i], n1_b[i])
            qkv = xn @ qkv_w[i].T
            q, k, v = jnp.split(qkv, 3, axis=-1)
            q = _rope(q.reshape(B, L, H, HD))
            k = _rope(k.reshape(B, L, H, HD))
            v = v.reshape(B, L, H, HD)
            a = _attn(q, k, v, src_mask).reshape(B, L, D) @ so_w[i].T
            x = x + a
            xn = _adaln(x, noise_emb, n2_w[i], n2_b[i])
            q = _rope((xn @ cq_w[i].T).reshape(B, L, H, HD))
            k = _rope((context @ ck_w[i].T).reshape(B, LC, H, HD))
            v = (context @ cv_w[i].T).reshape(B, LC, H, HD)
            a = _attn(q, k, v, ctx_mask).reshape(B, L, D) @ co_w[i].T
            x = x + a
            xn = _adaln(x, noise_emb, n3_w[i], n3_b[i])
            h = jax.nn.gelu(xn @ f1_w[i].T + f1_b[i], approximate=False)
            x = x + (h @ f2_w[i].T + f2_b[i])
        return x

    def _L0_ffn_ref(x, router_w, router_b, w1, b1, w2, b2):
        import math
        import jax, jax.numpy as jnp
        import numpy as np
        E = 8
        K = 2
        CF = 1.25
        D = 256
        F = 512
        B, S = (4, 512)
        b, s, d = x.shape
        xf = x.reshape(-1, d)
        T = b * s
        A = T * K
        cap = max(1, int(math.ceil(CF * A / E)))
        logits = xf @ router_w + router_b
        probs = jax.nn.softmax(logits, axis=-1)
        topk_p, topk_i = jax.lax.top_k(probs, K)
        topk_p = topk_p / jnp.clip(topk_p.sum(-1, keepdims=True), 1e-09)
        a_tok = jnp.repeat(jnp.arange(T), K)
        a_exp = topk_i.reshape(-1)
        a_w = topk_p.reshape(-1)
        order = jnp.argsort(a_exp)
        se, st, sw = (a_exp[order], a_tok[order], a_w[order])
        counts = jnp.bincount(se, length=E)
        starts = jnp.cumsum(counts) - counts
        rank = jnp.arange(A) - starts[se]
        keep = rank < cap
        slot = jnp.where(keep, se * cap + rank, E * cap)
        buf = jnp.zeros((E * cap + 1, d), x.dtype).at[slot].set(xf[st])
        buf = buf[:-1].reshape(E, cap, d)
        h = jax.nn.gelu(jnp.einsum('ecd,edf->ecf', buf, w1) + b1[:, None, :], approximate=False)
        eo = jnp.einsum('ecf,efd->ecd', h, w2) + b2[:, None, :]
        eo_flat = jnp.concatenate([eo.reshape(E * cap, d), jnp.zeros((1, d), x.dtype)], axis=0)
        w = jnp.where(keep, sw, 0.0)[:, None]
        out = jnp.zeros_like(xf).at[st].add(eo_flat[slot] * w)
        return out.reshape(b, s, d)
    x = x + _L0_xcond_ref(_layernorm(x, axis=-1), cond_1024[:, None, :], ctx_1024, mask_BxS_bf0, mask_BxS2_bf0, L0_xcond_n1_w, L0_xcond_n1_b, L0_xcond_n2_w, L0_xcond_n2_b, L0_xcond_n3_w, L0_xcond_n3_b, L0_xcond_qkv_w, L0_xcond_so_w, L0_xcond_cq_w, L0_xcond_ck_w, L0_xcond_cv_w, L0_xcond_co_w, L0_xcond_f1_w, L0_xcond_f1_b, L0_xcond_f2_w, L0_xcond_f2_b)
    x = x + _L0_ffn_ref(_layernorm(x, axis=-1), L0_ffn_router_w, L0_ffn_router_b, L0_ffn_w1, L0_ffn_b1, L0_ffn_w2, L0_ffn_b2)
    return x

_drawn_inputs = setup_inputs


def setup_inputs(seed=0):
    import zlib

    import numpy as np

    out = dict(_drawn_inputs(seed))
    spreads = {'L0_xcond_n1_b': (0.0, 0.32),
     'L0_xcond_n2_b': (0.0, 0.8),
     'L0_xcond_n3_b': (0.0, 0.1),
     'L0_xcond_f1_b': (0.0, 0.1),
     'L0_xcond_f2_b': (0.0, 0.1),
     'L0_ffn_router_b': (0.0, 0.1)}
    factors = {'L0_xcond_n2_w': 8.0,
     'L0_xcond_cq_w': 8.0,
     'L0_xcond_ck_w': 8.0,
     'L0_ffn_b1': 24.095,
     'L0_ffn_b2': 8.0}
    for name, (base, spread) in spreads.items():
        noise = np.random.default_rng([zlib.crc32(name.encode()), seed]).standard_normal(out[name].shape)
        drawn = base * np.exp(spread * noise) if base else spread * noise
        out[name] = jnp.asarray(drawn.astype(out[name].dtype))
    for name, factor in factors.items():
        out[name] = (out[name] * factor).astype(out[name].dtype)
    return out
```

```python
from contextlib import ExitStack

import numpy as np
import concourse.bass as bass
from concourse import mybir

F32, BF16, U8, U32 = mybir.dt.float32, mybir.dt.bfloat16, mybir.dt.uint8, mybir.dt.uint32
ALU, ACT, AX = mybir.AluOpType, mybir.ActivationFunctionType, mybir.AxisListType.X

NL, D, H, DFF, HD = 6, 256, 16, 1024, 16
B, S = 4, 512
T = B * S
NE, FE, CAP = 8, 512, 640
P = 128
KD = D // P
TT = S // P
NT = T // P
NJ = 2 * B
EPS = 1e-5
RING2 = 3
SLOT_UNITS = 16
MASKED = -3.0e38
Q_PARTS = (0, 0, 0, 1, 1, 2)
K_PARTS = (0, 1, 2, 0, 1, 0)
NPROD = len(Q_PARTS)
MASK_ROW = NPROD * HD
SHIFT_ROW = MASK_ROW + 1
ROWS = SHIFT_ROW + 2
VROW = H * (HD + 1) + HD
FT = DFF // P
CHUNKS_PER_LAYER = 192
DVE_PER_LAYER = 196
EXP_SET = "natural_log_exp_and_others"


class Place:

    def __init__(self):
        self.layer = 0

    def at(self, count, per_layer):
        return count + self.layer * per_layer

    def jobs(self, k, per_job):
        return self.at(k * per_job, NJ * per_job)


def is_cross(k):
    return k % NJ >= B


def run_slots(eng, place, head0, slot):
    head0()
    slot(0, p2=False, p1=True, tail=False, head=True)
    slot(1, p2=True, p1=True, tail=False, head=True)
    with eng.Fori(0, NL - 1) as layer:
        place.layer = layer
        for k in range(2, 2 + NJ):
            slot(k, p2=True, p1=True, tail=True, head=True)
    place.layer = NL - 2
    for k in range(2 + NJ, 2 * NJ):
        slot(k, p2=True, p1=True, tail=True, head=k + 1 < 2 * NJ)
    slot(2 * NJ, p2=True, p1=False, tail=True, head=False)
    slot(2 * NJ + 1, p2=False, p1=False, tail=True, head=False)


def build(nc, a, out):
    with ExitStack() as top:
        sb = lambda name, shape, dt=F32: top.enter_context(nc.sbuf_tensor(name, shape, dt))
        x = sb("x", [P, NT, D])
        mod = sb("mod", [P, 3 * NL, 4, B])
        ident = sb("ident", [P, P])
        identb = sb("identb", [P, P], BF16)
        eps = sb("eps", [P, 1])
        maskrow = sb("maskrow", [2 * B, S], BF16)
        prepare(nc, a, x, mod, ident, identb, eps, maskrow)
        layers(nc, a, x, mod, ident, identb, eps, maskrow)
        experts(nc, a, x, ident, eps, out)


def prepare(nc, a, x, mod, ident, identb, eps, maskrow):
    with ExitStack() as ctx:
        sb = lambda name, shape, dt=F32: ctx.enter_context(nc.sbuf_tensor(name, shape, dt))
        sem = lambda name: ctx.enter_context(nc.semaphore(name))
        NN = 3 * NL
        NG = -(-NN // 4)
        condT = sb("condT", [P, KD, 32])
        nw = sb("nw", [P, NN // 2, KD, 2 * D])
        nb = sb("nb", [P, NN, 4])
        gb = sb("gb", [P, NG, 2 * D])
        mask8 = sb("mask8", [2 * B, S // 4], U32)
        st = sb("pst", [P, NT, 6])
        mv = sb("pmv", [P, NT, 2])
        lnv = sb("plnv", [P, NT])
        y0 = sb("py0", [P, NT])
        ve = sb("pve", [P, NT])
        t1 = sb("pt1", [P, NT])
        ps = ctx.enter_context(nc.psum_tensor("pps", [P, 8, 512], F32))
        s_const = sem("p_const")
        s_cond = sem("p_cond")
        s_condz = sem("p_condz")
        s_nw = sem("p_nw")
        s_nw2 = sem("p_nw2")
        s_nb = sem("p_nb")
        s_mask = sem("p_mask")
        s_x = sem("p_x")
        s_gb = sem("p_gb")
        s_gbc = sem("p_gbc")
        s_gbT = sem("p_gbT")
        s_gbfree = sem("p_gbfree")
        s_rs = sem("p_rs")
        s_d = sem("p_dve")
        blk = ctx.enter_context(nc.Block())
        half = NN // 2

        @blk.sync
        def _(sp):
            sp.dma_start(x[:, :, :], a["x"].rearrange("(t p) d -> p t d", p=P)).then_inc(s_x, 16)
            sp.wait_ge(s_condz, 1)
            sp.dma_start(condT[:, :, 0:B], a["condT"].rearrange("(k p) b -> p k b", p=P)).then_inc(s_cond, 16)
            sp.dma_start(mask8[0:B, :], a["mask"]).then_inc(s_mask, 16)
            sp.dma_start(mask8[B:2 * B, :], a["mask2"]).then_inc(s_mask, 16)
            sp.dma_start(nb[:, :, :], a["nb"]).then_inc(s_nb, 16)
            for i in range(half):
                sp.dma_start(nw[:, i, :, :], a["nwT"][i].rearrange("(k p) o -> p k o", p=P)).then_inc(s_nw, 16)
            sp.wait_ge(s_gb, half)
            for i in range(half, NN):
                sp.dma_start(nw[:, i - half, :, :], a["nwT"][i].rearrange("(k p) o -> p k o", p=P)).then_inc(s_nw2, 16)

        @blk.gpsimd
        def _(pool):
            pool.memset(condT[:, :, :], 0.0).then_inc(s_condz, 1)
            pool.memset(ident[:, :], 0.0).then_inc(s_const, 1)
            pool.memset(identb[:, :], 0.0).then_inc(s_const, 1)
            pool.memset(eps[:, :], EPS).then_inc(s_const, 1)
            pool.wait_ge(s_const, 3)
            for m in (ident, identb):
                pool.affine_select(out=m[:, :], in_=m[:, :], compare_op=ALU.not_equal, fill=1.0, base=0,
                                   pattern=[[-1, P]], channel_multiplier=1).then_inc(s_const, 1)

        @blk.tensor
        def _(pe):
            pe.wait_ge(s_cond, 16)
            pe.wait_ge(s_nw, 16 * half)
            for i in range(4 * NG):
                if i == half:
                    pe.wait_ge(s_nw2, 16 * (NN - half))
                j = i % 4
                src = min(i, NN - 1) % half
                for k in range(KD):
                    mm = nc.tensor.matmul(ps[32 * j:32 * j + 32, i // 4, :], condT[:, k, :], nw[:, src, k, :],
                                          start=(k == 0), stop=(k == KD - 1))
                mm.then_inc(s_gb, 1)
            pe.wait_ge(s_const, 5)
            for g in range(NG):
                pe.wait_ge(s_gbc, g + 1)
                if g >= 2:
                    pe.wait_ge(s_gbfree, g - 1)
                for m in range(4):
                    tr = nc.tensor.transpose(ps[:, 5 + g % 2, m * P:(m + 1) * P], gb[:, g, m * P:(m + 1) * P], ident[:, :])
                tr.then_inc(s_gbT, 1)

        @blk.scalar
        def _(act):
            act.preload_act_table_set(EXP_SET)
            for g in range(NG):
                act.wait_ge(s_gb, 4 * g + 4)
                nc.scalar.activation(gb[:, g, :], ps[:, g, :], ACT.Copy).then_inc(s_gbc, 1)
            act.wait_ge(s_const, 5)
            act.wait_ge(s_rs, 1)
            nc.scalar.activation(lnv[:, :], mv[:, :, 1], ACT.Ln, bias=eps[:, 0:1]).then_inc(s_rs, 1)
            act.wait_ge(s_rs, 2)
            nc.scalar.activation(y0[:, :], lnv[:, :], ACT.Exp, scale=-0.5).then_inc(s_rs, 1)

        @blk.vector
        def _(dve):
            n = [0]

            def link(ins):
                n[0] += 1
                ins.then_inc(s_d, 1)
                dve.wait_ge(s_d, n[0])

            dve.wait_ge(s_mask, 32)
            nc.vector.tensor_scalar(maskrow[:, :], mask8[:, :].bitcast(U8), MASKED, None, ALU.mult).then_inc(s_d, 1)
            n[0] += 1
            dve.wait_ge(s_x, 16)
            for t in range(NT):
                ins = nc.vector.bn_stats(st[:, t, :], x[:, t, :])
                ins.then_inc(s_d, 1)
            n[0] += NT
            dve.wait_ge(s_d, n[0])
            for t in range(NT):
                nc.vector.bn_aggr(mv[:, t, :], st[:, t, :]).then_inc(s_d, 1)
            n[0] += NT
            dve.wait_ge(s_d, n[0])
            nc.vector.tensor_scalar(ve[:, :], mv[:, :, 1], EPS, None, ALU.add).then_inc(s_rs, 1)
            dve.wait_ge(s_rs, 3)
            link(nc.vector.scalar_tensor_tensor(t1[:, :], y0[:, :], -0.5, y0[:, :], ALU.mult, ALU.mult))
            link(nc.vector.tensor_tensor(t1[:, :], t1[:, :], ve[:, :], ALU.mult))
            link(nc.vector.scalar_tensor_tensor(y0[:, :], t1[:, :], 1.5, y0[:, :], ALU.add, ALU.mult))
            for t in range(NT):
                ins = nc.vector.tensor_scalar(x[:, t, :], x[:, t, :], mv[:, t, 0:1], y0[:, t:t + 1],
                                              ALU.subtract, ALU.mult)
                ins.then_inc(s_d, 1)
            n[0] += NT
            dve.wait_ge(s_nb, 16)
            for g in range(NG):
                dve.wait_ge(s_gbT, g + 1)
                w = min(4, NN - 4 * g)
                for m in range(4):
                    src = ps[:, 5 + g % 2, m * P:m * P + 32 * w].rearrange("p (j c) -> p j c", j=w)[:, :, 0:B]
                    ins = nc.vector.tensor_tensor(mod[:, 4 * g:4 * g + w, m, :], src,
                                                  nb[:, 4 * g:4 * g + w, m:m + 1].to_broadcast([P, w, B]), ALU.add)
                    if m == 3:
                        ins.then_inc(s_gbfree, 1)
                    else:
                        ins.then_inc(s_d, 1)
                        n[0] += 1
            dve.wait_ge(s_gbfree, NG)
            dve.wait_ge(s_d, n[0])
            link(nc.vector.tensor_scalar(mod[:, :, 0:2, :], mod[:, :, 0:2, :], 1.0, None, ALU.add))


def layers(nc, a, x, mod, ident, identb, eps, maskrow):
    with ExitStack() as ctx:
        sb = lambda name, shape, dt=F32: ctx.enter_context(nc.sbuf_tensor(name, shape, dt))
        sem = lambda name: ctx.enter_context(nc.semaphore(name))
        wself = sb("wself", [P, 4, KD, D])
        wcross = sb("wcross", [P, 4, KD, D])
        wf1 = sb("wf1", [P, KD, DFF])
        wf2 = sb("wf2", [P, FT, D])
        f1b = sb("f1b", [P, FT])
        f2b = sb("f2b", [P, D])
        qs = [sb(f"qstack{i}", [ROWS, H, S], BF16) for i in range(2)]
        ks = [sb(f"kstack{i}", [ROWS, H, S], BF16) for i in range(2)]
        parts = sb("parts", [P, 3, KD, S], BF16)
        ropep = sb("ropep", [P, 4, S])
        rot = sb("rot", [P, KD, S])
        prob = sb("prob", [P, 8, S])
        v = [sb(f"v{b}", [P, TT, VROW]) for b in range(B)]
        xnT = sb("xnT", [P, KD, S])
        xnat = sb("xnat", [P, TT, D])
        ctxT = sb("ctxT", [P, KD, S])
        osum = sb("osum", [P, 4, S])
        anat = sb("anat", [P, TT, D])
        hT = sb("hT", [P, FT, S // 2])
        aT = hT[:, 0:4, :].rearrange("p (k a) n -> p k (a n)", k=KD)
        cos = sb("cos", [P, S])
        sin = sb("sin", [P, S])
        negmax = sb("negmax", [P, 2, TT, H // 2])
        mres = sb("mres", [P, 2, TT, H // 2])
        mpart = sb("mpart", [P, 2, TT, 2, H // 2], BF16)
        mrow = sb("mrow", [16, 2, S], BF16)
        recip = sb("recip", [P, TT, H])
        st = sb("st", [P, TT, 6])
        mv = sb("mv", [P, TT, 2])
        lnv = sb("lnv", [P, TT])
        y0 = sb("y0", [P, TT])
        ve = sb("ve", [P, TT])
        fence_at = sb("fence_at", [P, 1])
        bounce = [nc.dram_tensor(f"bounce{i}", (3, D, S), BF16, kind="Internal").ap() for i in range(2)]

        psum = lambda name, n: ctx.enter_context(nc.psum_tensor(name, [P, n, 512], F32))
        ps1 = psum("ps1", 2)
        ps2 = psum("ps2", RING2)
        psv = psum("psv", 1)
        side = psum("side", 2)

        s_wself = sem("wself_loaded")
        s_wcross = sem("wcross_loaded")
        s_wffn = sem("wffn_loaded")
        s_table = sem("tables_loaded")
        s_ctx = sem("context_loaded")
        s_bounce = [sem(f"bounce_written{i}") for i in range(2)]
        s_stack = [sem(f"stack_loaded{i}") for i in range(2)]
        s_mload = [sem(f"shift_loaded{i}") for i in range(2)]
        s_init = sem("constants_set")
        s_p1full = sem("scores_ready")
        s_p1free = sem("scores_reduced")
        s_p2full = sem("shifted_ready")
        s_prob = sem("probs_ready")
        s_pv = sem("pv_unit_done")
        s_os = sem("pv_group_copied")
        s_full = sem("chunk_filled")
        s_read = [sem(f"chunk_read{i}") for i in range(2)]
        s_var = sem("variance_ready")
        s_ln = sem("log_ready")
        s_guess = sem("rstd_guess_ready")
        s_xnat = sem("normed_ready")
        s_rot = sem("rope_done")
        s_hi = sem("high_part_ready")
        s_r1 = sem("high_residual_ready")
        s_mid = sem("mid_part_ready")
        s_low = sem("low_part_ready")
        s_mpart = sem("shift_parts_ready")
        s_bias = sem("ffn_bias_added")
        s_dve = sem("dve_step")
        blk = ctx.enter_context(nc.Block())

        STACK_DMAS = 16 * (2 * NPROD + 1)

        def slot_chunks(k):
            p2, p1 = 1 <= k <= 2 * NJ, k < 2 * NJ
            tail, head = k >= 2, k + 1 < 2 * NJ
            ffn = tail and is_cross(k - 2)
            plan = {u: [] for u in range(SLOT_UNITS)}
            if k == -1:
                plan[0] = [(w, c) for w in ("HT", "HQ", "HK", "HV") for c in range(2)]
                return plan
            if tail:
                plan[0] += [("T1", 0), ("T1", 1)]
                plan[1] += [("T1", 2), ("T1", 3)]
            if p2:
                plan[1] += [("M", 1)]
            if head:
                plan[2] += [("HT", 0), ("HT", 1)]
            if tail:
                plan[3] += [("T2", 0), ("T2", 1)]
            if head:
                plan[4] += [("HQ", 0), ("HQ", 1)]
            if tail:
                plan[5] += [("O", 0), ("O", 1)]
            if head:
                plan[6] += [("HK", 0), ("HK", 1)]
                plan[7] += [("HV", 0), ("HV", 1)]
            if ffn:
                plan[8] += [("LT", 0), ("LT", 1)]
            if p1:
                plan[9] += [("M", 0)]
            if ffn:
                plan[11] += [("F1", c) for c in range(4)]
                plan[12] += [("F2", 0)]
                plan[14] += [("F1", c) for c in range(4, 8)]
                plan[15] += [("F2", 1)]
            return plan

        number, start = {}, {}
        for k in range(-1, 2 * NJ + 2):
            start[k] = len(number)
            for u, names in slot_chunks(k).items():
                for name in names:
                    number[(k, *name)] = len(number)
        assert start[2 + NJ] - start[2] == CHUNKS_PER_LAYER

        def wait_filled(eng, place, k, what, c):
            eng.wait_ge(s_full, place.at(number[(k, what, c)] + 1, CHUNKS_PER_LAYER))

        def wait_read(eng, place, k, what, c):
            n = number[(k, what, c)]
            eng.wait_ge(s_read[n % 2], place.at(n // 2 + 1, CHUNKS_PER_LAYER // 2))

        def bank_of(k, what, c):
            n = number[(k, what, c)]
            return side[:, n % 2, :], s_read[n % 2]

        def cross_before(j):
            return (j // NJ) * B + max(0, j % NJ - B) if j > 0 else 0

        def norm_index(k, what):
            return min(k + 1, 2 * NJ) + (what == "LT" and k + 1 < 2 * NJ) + cross_before(k - 2)

        def norms(place, k, what, add=0):
            return place.at(norm_index(k, what) + add, NJ + B)

        def norm_row(k, what):
            if what == "LT":
                j = k - 2
                return 3 * (j // NJ) + 2, j % B
            j = k + 1
            return 3 * (j // NJ) + (1 if is_cross(j) else 0), j % B

        @blk.sync
        def _(sp):
            place = Place()

            def at_layer(name, k):
                layer = place.layer + k // NJ
                ap = a[name]
                return ap[bass.ds(layer, 1)] if not isinstance(layer, int) else ap[layer:layer + 1]

            def load_self(k):
                for i in range(4):
                    sp.dma_start(wself[:, i, :, :], at_layer("wself", k)[:, i].rearrange("l (k p) o -> p (l k) o", p=P)).then_inc(s_wself, 16)

            def load_cross_ffn(k):
                for i in range(4):
                    sp.dma_start(wcross[:, i, :, :], at_layer("wcross", k)[:, i].rearrange("l (k p) o -> p (l k) o", p=P)).then_inc(s_wcross, 16)
                sp.dma_start(wf1[:, :, :], at_layer("f1T", k).rearrange("l (k p) o -> p (l k) o", p=P)).then_inc(s_wffn, 16)
                sp.dma_start(wf2[:, :, :], at_layer("f2T", k).rearrange("l (k p) o -> p (l k) o", p=P)).then_inc(s_wffn, 16)
                sp.dma_start(f1b[:, :], at_layer("f1b", k).rearrange("l p f -> p (l f)")).then_inc(s_wffn, 16)
                sp.dma_start(f2b[:, :], at_layer("f2b", k).to_broadcast([P, D])).then_inc(s_wffn, 16)

            def shift_rows(k, j, hf):
                wait_read(sp, place, k, "M", hf)
                for r in range(2):
                    sp.dma_start(qs[j % 2][SHIFT_ROW + r:SHIFT_ROW + r + 1, 8 * hf:8 * hf + 8, :],
                                 mrow[8 * r:8 * r + 8, hf, :]).then_inc(s_mload[hf], 16)

            def write_parts(j):
                for w in range(2):
                    if j > 0 and w == 0:
                        for hf in range(2):
                            sp.wait_ge(s_stack[hf], place.jobs(j, STACK_DMAS))
                    sp.wait_ge(s_low, place.jobs(j, 2) + w + 1)
                    sp.dma_start(bounce[w].rearrange("r (t p) n -> p (r t) n", p=P),
                                 parts[:, :, :, :].rearrange("p r t n -> p (r t) n")).then_inc(s_bounce[w], 16)

            def load_stack(j, hf):
                if hf == 0:
                    for w in range(2):
                        sp.wait_ge(s_bounce[w], place.jobs(j + 1, 16))
                if j >= 2:
                    sp.wait_ge(s_p2full, place.jobs(j - 2, 64) + 32 * (hf + 1))
                heads = slice(8 * hf, 8 * hf + 8)
                for w, (stack, order) in enumerate(((qs, Q_PARTS), (ks, K_PARTS))):
                    for r, part in enumerate(order):
                        sp.dma_start(stack[j % 2][HD * r:HD * (r + 1), heads, :],
                                     bounce[w][part].rearrange("(c h) n -> c h n", h=H)[:, heads, :]).then_inc(s_stack[hf], 16)
                row = j % NJ
                sp.dma_start(ks[j % 2][MASK_ROW:MASK_ROW + 1, heads, :],
                             maskrow[row:row + 1, None, :].to_broadcast([1, 8, S])).then_inc(s_stack[hf], 16)

            def head0():
                load_self(0)
                sp.dma_start(cos[:, :], a["cos"]).then_inc(s_table, 16)
                sp.dma_start(sin[:, :], a["sin"]).then_inc(s_table, 16)
                sp.wait_ge(s_init, 4)
                write_parts(0)
                load_stack(0, 0)
                load_stack(0, 1)

            def slot(k, p2, p1, tail, head):
                side_done = place.at(start[k], CHUNKS_PER_LAYER)
                if k % NJ == 2 and p1:
                    sp.wait_ge(s_full, side_done)
                    load_cross_ffn(k)
                if head and is_cross(k + 1):
                    sp.wait_ge(s_full, side_done)
                    b = (k + 1) % B
                    sp.dma_start(ctxT[:, :, :], a["ctxT"].rearrange("(k p) n -> p k n", p=P)[:, :, b * S:(b + 1) * S]).then_inc(s_ctx, 16)
                if k % NJ == 6 and k < NJ:
                    sp.wait_ge(s_full, side_done)
                    load_self(k + NJ)
                if p2:
                    shift_rows(k, k - 1, 1)
                if head:
                    write_parts(k + 1)
                    load_stack(k + 1, 0)
                if p1:
                    shift_rows(k, k, 0)
                if head:
                    load_stack(k + 1, 1)

            run_slots(sp, place, head0, slot)

        @blk.gpsimd
        def _(pool):
            place = Place()
            for i in range(2):
                pool.memset(qs[i][MASK_ROW:ROWS, :, :], 1.0).then_inc(s_init, 1)
                pool.memset(ks[i][MASK_ROW:ROWS, :, :], 1.0).then_inc(s_init, 1)
            pool.wait_ge(s_init, 4)
            for b in range(B):
                pool.memset(v[b][:, :, :], 1.0).then_inc(s_init, 1)

            def split(k, j, w):
                done = place.jobs(j, 2) + w
                wait_read(pool, place, k, ("HQ", "HK")[w], 1)
                if j or w:
                    pool.wait_ge(s_mid, done)
                    pool.wait_ge(s_low, done)
                nc.gpsimd.tensor_tensor(rot[:, 0, :], ropep[:, 0, :], ropep[:, 1, :], ALU.subtract).then_inc(s_rot, 1)
                nc.gpsimd.tensor_tensor(rot[:, 1, :], ropep[:, 2, :], ropep[:, 3, :], ALU.add).then_inc(s_rot, 1)
                pool.wait_ge(s_hi, done + 1)
                nc.gpsimd.tensor_tensor(rot[:, :, :], rot[:, :, :], parts[:, 0, :, :], ALU.subtract).then_inc(s_r1, 1)
                pool.wait_ge(s_mid, done + 1)
                nc.gpsimd.tensor_tensor(parts[:, 2, :, :], rot[:, :, :], parts[:, 1, :, :], ALU.subtract).then_inc(s_low, 1)

            def head0():
                split(-1, 0, 0)
                split(-1, 0, 1)

            def slot(k, p2, p1, tail, head):
                if head:
                    split(k, k + 1, 0)
                    split(k, k + 1, 1)
                if tail and is_cross(k - 2):
                    j = k - 2
                    tiles = slice(TT * (j % B), TT * (j % B + 1))
                    pool.wait_ge(s_xnat, norms(place, k, "LT", 1))
                    pool.wait_ge(s_wffn, place.at(64 * (j // NJ + 1), 64))
                    nc.gpsimd.tensor_tensor(x[:, tiles, :], x[:, tiles, :], f2b[:, None, :].to_broadcast([P, TT, D]),
                                            ALU.add).then_inc(s_bias, 1)

            run_slots(pool, place, head0, slot)

        @blk.tensor
        def _(pe):
            place = Place()

            def begin(k, what, c):
                n = number[(k, what, c)]
                if n >= 2:
                    pe.wait_ge(s_read[n % 2], place.at(n // 2, CHUNKS_PER_LAYER // 2))
                return side[:, n % 2, :]

            def transposes(bank, tiles):
                for i, tile in enumerate(tiles):
                    tr = nc.tensor.transpose(bank[:, i * P:(i + 1) * P], tile, ident[:, :])
                tr.then_inc(s_full, 1)

            def project_T(bank, w, act_T, m):
                for k in range(KD):
                    mm = nc.tensor.matmul(bank, w[:, k, m * P:(m + 1) * P], act_T[:, k, :], start=(k == 0), stop=(k == KD - 1))
                mm.then_inc(s_full, 1)

            def project(bank, w, act_T, t0, nk):
                for i in range(2):
                    t = t0 + i
                    for k in range(nk):
                        mm = nc.tensor.matmul(bank[:, i * D:(i + 1) * D], act_T[:, k, t * P:(t + 1) * P], w[:, k, :],
                                              start=(k == 0), stop=(k == nk - 1))
                mm.then_inc(s_full, 1)

            def side_work(k, what, c):
                if what == "T1":
                    if c == 0:
                        pe.wait_ge(s_os, place.jobs(k - 1, 4))
                    transposes(begin(k, what, c), [osum[:, g, c * P:(c + 1) * P] for g in range(4)])
                elif what == "T2":
                    if c == 0:
                        wait_read(pe, place, k, "T1", 2)
                        wait_read(pe, place, k, "T1", 3)
                    transposes(begin(k, what, c), [anat[:, t, c * P:(c + 1) * P] for t in range(TT)])
                elif what == "O":
                    if c == 0:
                        wait_read(pe, place, k, "T2", 0)
                        wait_read(pe, place, k, "T2", 1)
                    w = wcross if is_cross(k - 2) else wself
                    project(begin(k, what, c), w[:, 3], aT, 2 * c, KD)
                elif what in ("HT", "LT"):
                    if c == 0:
                        pe.wait_ge(s_xnat, norms(place, k, what, 1))
                    transposes(begin(k, what, c), [xnat[:, t, c * P:(c + 1) * P] for t in range(TT)])
                elif what in ("HQ", "HK", "HV"):
                    j = k + 1
                    i = ("HQ", "HK", "HV").index(what)
                    if i == 0 and c == 0:
                        wait_read(pe, place, k, "HT", 0)
                        wait_read(pe, place, k, "HT", 1)
                        pe.wait_ge(s_wcross if is_cross(j) else s_wself, place.at(64 * (j // NJ + 1), 64))
                    if i == 1 and c == 0 and is_cross(j):
                        pe.wait_ge(s_ctx, place.at(16 * (cross_before(j) + 1), 16 * B))
                    src = ctxT if is_cross(j) and i > 0 else xnT
                    w = (wcross if is_cross(j) else wself)[:, i]
                    if i < 2:
                        project_T(begin(k, what, c), w, src, c)
                    else:
                        project(begin(k, what, c), w, src, 2 * c, KD)
                elif what == "M":
                    j = k - 1 if c == 1 else k
                    pe.wait_ge(s_mpart, place.jobs(j, 2) + c + 1)
                    bank = begin(k, what, c)
                    for t in range(TT):
                        mm = nc.tensor.matmul(bank[0:16, t * P:(t + 1) * P], mpart[:, c, t, :, :].rearrange("p a b -> p (a b)"),
                                              identb[:, :], start=True, stop=True)
                    mm.then_inc(s_full, 1)
                elif what == "F1":
                    th, cc = divmod(c, 4)
                    if c == 0:
                        wait_read(pe, place, k, "LT", 0)
                        wait_read(pe, place, k, "LT", 1)
                        pe.wait_ge(s_wffn, place.at(64 * ((k - 2) // NJ + 1), 64))
                    bank = begin(k, what, c)
                    for i in range(2):
                        f = 2 * cc + i
                        for kk in range(KD):
                            mm = nc.tensor.matmul(bank[:, i * D:(i + 1) * D], wf1[:, kk, f * P:(f + 1) * P],
                                                  xnT[:, kk, th * (S // 2):(th + 1) * (S // 2)],
                                                  start=(kk == 0), stop=(kk == KD - 1))
                    mm.then_inc(s_full, 1)
                elif what == "F2":
                    wait_read(pe, place, k, "F1", 4 * c + 2)
                    wait_read(pe, place, k, "F1", 4 * c + 3)
                    project(begin(k, what, c), wf2, hT, 0, FT)

            def pass2(j, u):
                g, kt = divmod(u, TT)
                q, kk = qs[j % 2], ks[j % 2]
                if u % 8 == 0:
                    pe.wait_ge(s_mload[u // 8], place.jobs(j + 1, 32))
                for i in range(4):
                    h, n = 4 * g + i, 4 * u + i
                    back = n - 2 if j % NJ or n > 1 else n - 1
                    if j > 0 or n >= RING2:
                        pe.wait_ge(s_prob, place.jobs(j, 64) + back)
                    nc.tensor.matmul(ps2[:, (n + j % NJ) % RING2, :], kk[:, h, kt * P:(kt + 1) * P], q[:, h, :],
                                     start=True, stop=True).then_inc(s_p2full, 1)

            def pv(j, u):
                g, kt = divmod(u, TT)
                if kt == 0 and (j > 0 or u > 0):
                    pe.wait_ge(s_os, place.jobs(j, 4) + g)
                pe.wait_ge(s_prob, place.jobs(j, 64) + 4 * u + 4)
                for i in range(4):
                    h = 4 * g + i
                    mm = nc.tensor.matmul(psv[32 * i:32 * i + 32, 0, :], v[j % B][:, kt, (HD + 1) * h:(HD + 1) * h + 32],
                                          prob[:, 4 * (u % 2) + i, :], start=(kt == 0), stop=(kt == TT - 1))
                mm.then_inc(s_pv, 1)

            def pass1(j, h):
                if h % 8 == 0:
                    pe.wait_ge(s_stack[h // 8], place.jobs(j + 1, STACK_DMAS))
                q, kk = qs[j % 2], ks[j % 2]
                for t in range(TT):
                    n = TT * h + t
                    if j > 0 or n >= 2:
                        pe.wait_ge(s_p1free, place.jobs(j, 64) + n - 1)
                    nc.tensor.matmul(ps1[:, n % 2, :], q[0:SHIFT_ROW, h, t * P:(t + 1) * P], kk[0:SHIFT_ROW, h, :],
                                     start=True, stop=True).then_inc(s_p1full, 1)

            def head0():
                pe.wait_ge(s_init, 8)
                for what, c in slot_chunks(-1)[0]:
                    side_work(-1, what, c)

            def slot(k, p2, p1, tail, head):
                plan = slot_chunks(k)
                for u in range(SLOT_UNITS):
                    if p2:
                        pass2(k - 1, u)
                        if u:
                            pv(k - 1, u - 1)
                    if p1:
                        pass1(k, u)
                    for what, c in plan[u]:
                        side_work(k, what, c)
                if p2:
                    pv(k - 1, SLOT_UNITS - 1)

            run_slots(pe, place, head0, slot)

        @blk.scalar
        def _(act):
            place = Place()
            act.preload_act_table_set(EXP_SET)

            def exps(j, u):
                for i in range(4):
                    n = 4 * u + i
                    act.wait_ge(s_p2full, place.jobs(j, 64) + n + 1)
                    if i == 0 and (j > 0 or u >= 2):
                        act.wait_ge(s_pv, place.jobs(j, 16) + u - 1)
                    nc.scalar.activation(prob[:, 4 * (u % 2) + i, :], ps2[:, (n + j % NJ) % RING2, :], ACT.Exp,
                                         scale=HD ** -0.5).then_inc(s_prob, 1)

            def copy_group(k, j, g):
                if g == 0 and k >= 2:
                    wait_filled(act, place, k, "T1", 3)
                act.wait_ge(s_pv, place.jobs(j, 16) + 4 * g + 4)
                nc.scalar.activation(osum[:, g, :], psv[:, 0, :], ACT.Copy).then_inc(s_os, 1)

            def rstd_guess(k, what):
                act.wait_ge(s_var, norms(place, k, what, 1))
                nc.scalar.activation(lnv[:, :], mv[:, :, 1], ACT.Ln, bias=eps[:, 0:1]).then_inc(s_ln, 1)
                act.wait_ge(s_ln, norms(place, k, what, 1))
                nc.scalar.activation(y0[:, :], lnv[:, :], ACT.Exp, scale=-0.5).then_inc(s_guess, 1)

            def modulate(k, what, c):
                wait_filled(act, place, k, what, c)
                bank, read = bank_of(k, what, c)
                row, b = norm_row(k, what)
                layer = place.layer
                if isinstance(layer, int):
                    g = mod[:, row + 3 * layer, c, b:b + 1]
                    be = mod[:, row + 3 * layer, KD + c, b:b + 1]
                else:
                    i = layer * 3 + row
                    g = mod[:, bass.ds(i, 1), c, b:b + 1].rearrange("p a b -> p (a b)")
                    be = mod[:, bass.ds(i, 1), KD + c, b:b + 1].rearrange("p a b -> p (a b)")
                nc.scalar.activation(xnT[:, c, :], bank, ACT.Identity, scale=g, bias=be).then_inc(read, 1)

            def hi(j, w):
                done = place.jobs(j, 2) + w
                act.wait_ge(s_rot, place.jobs(j, 4) + 2 * w + 2)
                if w == 1:
                    act.wait_ge(s_bounce[0], place.jobs(j + 1, 16))
                elif j > 0:
                    act.wait_ge(s_bounce[1], place.jobs(j, 16))
                nc.scalar.activation(parts[:, 0, :, :], rot[:, :, :], ACT.Copy).then_inc(s_hi, 1)

            def mid(j, w):
                act.wait_ge(s_r1, place.jobs(j, 2) + w + 1)
                nc.scalar.activation(parts[:, 1, :, :], rot[:, :, :], ACT.Copy).then_inc(s_mid, 1)

            def side_work(k, what, c):
                if what in ("HT", "LT"):
                    modulate(k, what, c)
                elif what == "T2":
                    wait_filled(act, place, k, what, c)
                    bank, read = bank_of(k, what, c)
                    nc.scalar.activation(aT[:, c, :], bank, ACT.Copy).then_inc(read, 1)
                elif what == "HV":
                    wait_filled(act, place, k, what, c)
                    bank, read = bank_of(k, what, c)
                    j = k + 1
                    dst = v[j % B][:, 2 * c:2 * c + 2, 0:H * (HD + 1)].rearrange("p t (h e) -> p t h e", h=H)[:, :, :, 0:HD]
                    nc.scalar.activation(dst, bank.rearrange("p (t h d) -> p t h d", t=2, h=H), ACT.Copy).then_inc(read, 1)
                elif what == "F1":
                    wait_filled(act, place, k, what, c)
                    bank, read = bank_of(k, what, c)
                    for i in range(2):
                        f = 2 * (c % 4) + i
                        ins = nc.scalar.activation(hT[:, f, :], bank[:, i * D:(i + 1) * D], ACT.Gelu, bias=f1b[:, f:f + 1])
                    ins.then_inc(read, 1)
                    if c % 4 == 3:
                        act.preload_act_table_set(EXP_SET)

            def head0():
                rstd_guess(-1, "HT")
                for c in range(2):
                    modulate(-1, "HT", c)
                hi(0, 0)
                mid(0, 0)
                hi(0, 1)
                mid(0, 1)
                for c in range(2):
                    side_work(-1, "HV", c)

            def slot(k, p2, p1, tail, head):
                plan = slot_chunks(k)
                for u in range(SLOT_UNITS):
                    if p2:
                        exps(k - 1, u)
                        if u and u % TT == 0:
                            copy_group(k, k - 1, u // TT - 1)
                    for what, c in plan[u]:
                        side_work(k, what, c)
                    if head and u == 0:
                        rstd_guess(k, "HT")
                    if tail and is_cross(k - 2) and u == 6:
                        rstd_guess(k, "LT")
                    if head and u == 5:
                        hi(k + 1, 0)
                    if head and u == 6:
                        mid(k + 1, 0)
                    if head and u == 8:
                        hi(k + 1, 1)
                    if head and u == 9:
                        mid(k + 1, 1)
                if p2:
                    copy_group(k, k - 1, TT - 1)

            run_slots(act, place, head0, slot)

        @blk.vector
        def _(dve):
            place = Place()
            steps = [0]

            def step(ins):
                steps[0] += 1
                ins.then_inc(s_dve, 1)
                return steps[0]

            def wait_step(n):
                dve.wait_ge(s_dve, place.at(n, DVE_PER_LAYER))

            def stats(k, what):
                j = k - 2 if what == "LT" else k + 1
                if what == "LT":
                    wait_read(dve, place, k, "O", 1)
                elif steps[0]:
                    wait_step(steps[0])
                for t in range(TT):
                    n = step(nc.vector.bn_stats(st[:, t, :], x[:, TT * (j % B) + t, :]))
                wait_step(n)
                nc.vector.memset(fence_at[:, :], 0.0)
                for t in range(TT):
                    n = step(nc.vector.bn_aggr(mv[:, t, :], st[:, t, :]))
                wait_step(n)
                nc.vector.tensor_scalar(ve[:, :], mv[:, :, 1], EPS, None, ALU.add).then_inc(s_var, 1)

            def normalise(k, what):
                j = k - 2 if what == "LT" else k + 1
                dve.wait_ge(s_guess, norms(place, k, what, 1))
                wait_step(step(nc.vector.scalar_tensor_tensor(lnv[:, :], y0[:, :], -0.5, y0[:, :], ALU.mult, ALU.mult)))
                wait_step(step(nc.vector.tensor_tensor(lnv[:, :], lnv[:, :], ve[:, :], ALU.mult)))
                wait_step(step(nc.vector.scalar_tensor_tensor(y0[:, :], lnv[:, :], 1.5, y0[:, :], ALU.add, ALU.mult)))
                for t in range(TT):
                    ins = nc.vector.tensor_scalar(xnat[:, t, :], x[:, TT * (j % B) + t, :], mv[:, t, 0:1], y0[:, t:t + 1],
                                                  ALU.subtract, ALU.mult)
                ins.then_inc(s_xnat, 1)

            def maxima(j, h):
                for t in range(TT):
                    n = TT * h + t
                    dve.wait_ge(s_p1full, place.jobs(j, 64) + n + 1)
                    nc.vector.tensor_reduce(negmax[:, h // 8, t, h % 8:h % 8 + 1], ps1[:, n % 2, :], AX, ALU.max,
                                            negate=True).then_inc(s_p1free, 1)

            def shift_parts(j, hf):
                dve.wait_ge(s_p1free, place.jobs(j, 64) + 32 * (hf + 1))
                wait_step(step(nc.vector.tensor_copy(mpart[:, hf, :, 0, :], negmax[:, hf, :, :])))
                wait_step(step(nc.vector.tensor_tensor(mres[:, hf, :, :], negmax[:, hf, :, :], mpart[:, hf, :, 0, :], ALU.subtract)))
                nc.vector.tensor_copy(mpart[:, hf, :, 1, :], mres[:, hf, :, :]).then_inc(s_mpart, 1)

            def side_work(k, what, c):
                if what not in ("T1", "M", "HQ", "HK", "O", "F2"):
                    return
                wait_filled(dve, place, k, what, c)
                bank, read = bank_of(k, what, c)
                if what == "T1":
                    heads = bank.rearrange("p (h e) -> p h e", h=H)
                    wait_step(step(nc.vector.reciprocal(recip[:, c, :], heads[:, :, HD])))
                    nc.vector.tensor_tensor(anat[:, c, :].rearrange("p (h d) -> p h d", h=H), heads[:, :, 0:HD],
                                            recip[:, c, :, None].to_broadcast([P, H, HD]), ALU.mult).then_inc(read, 1)
                elif what == "M":
                    j = k - 1 if c == 1 else k
                    if j > 0:
                        dve.wait_ge(s_mload[c], place.jobs(j, 32))
                    nc.vector.tensor_copy(mrow[:, c, :], bank[0:16, :]).then_inc(read, 1)
                elif what in ("HQ", "HK"):
                    j, w = k + 1, int(what == "HK")
                    if c == 0:
                        if j == 0 and w == 0:
                            dve.wait_ge(s_table, 32)
                        else:
                            dve.wait_ge(s_rot, place.jobs(j, 4) + 2 * w)
                    first, second = (cos, sin) if c == 0 else (sin, cos)
                    nc.vector.tensor_tensor(ropep[:, c, :], bank, first[:, :], ALU.mult)
                    nc.vector.tensor_tensor(ropep[:, 2 + c, :], bank, second[:, :], ALU.mult).then_inc(read, 1)
                else:
                    j = k - 2
                    t0 = TT * (j % B) + 2 * c
                    if what == "F2" and c == 0:
                        dve.wait_ge(s_bias, place.at(cross_before(j) + 1, B))
                    nc.vector.tensor_tensor(x[:, t0:t0 + 2, :], x[:, t0:t0 + 2, :], bank.rearrange("p (t d) -> p t d", t=2),
                                            ALU.add).then_inc(read, 1)

            def head0():
                stats(-1, "HT")
                normalise(-1, "HT")
                for what, c in slot_chunks(-1)[0]:
                    side_work(-1, what, c)

            def slot(k, p2, p1, tail, head):
                if k == 2:
                    steps_at_loop[0] = steps[0]
                if k == 2 + NJ:
                    assert steps[0] - steps_at_loop[0] == DVE_PER_LAYER, steps[0] - steps_at_loop[0]
                plan = slot_chunks(k)
                ffn = tail and is_cross(k - 2)
                for u in range(SLOT_UNITS):
                    if head and u == 0:
                        stats(k, "HT")
                    if head and u == 1:
                        normalise(k, "HT")
                    if ffn and u == 6:
                        stats(k, "LT")
                    if ffn and u == 7:
                        normalise(k, "LT")
                    if p1:
                        maxima(k, u)
                    for what, c in plan[u]:
                        side_work(k, what, c)
                    if p1 and u == 7:
                        shift_parts(k, 0)
                if p1:
                    shift_parts(k, 1)

            steps_at_loop = [0]
            run_slots(dve, place, head0, slot)


def experts(nc, a, x, ident, eps, out):
    with ExitStack() as ctx:
        sb = lambda name, shape, dt=F32: ctx.enter_context(nc.sbuf_tensor(name, shape, dt))
        sem = lambda name: ctx.enter_context(nc.semaphore(name))
        xin = sb("xin", [P, NT, D])
        z = sb("z", [P, NT, D])
        zT = sb("zT", [P, KD, T])
        rw = sb("rw", [P, KD, NE])
        rb = sb("rb", [P, NE])
        b2 = sb("b2", [NE, D])
        b1 = sb("b1", [P, NE, FE // P])
        w1 = sb("w1", [P, 2, KD, FE])
        w2 = sb("w2", [P, 2, FE // P, D])
        hg = sb("hg", [P, 2, FE // P, S])
        st = sb("est", [P, NT, 6])
        mv = sb("emv", [P, NT, 2])
        lnv = sb("elnv", [P, NT])
        y0 = sb("ey0", [P, NT])
        ve = sb("eve", [P, NT])
        lg = sb("lg", [P, NT, NE])
        pr = sb("pr", [P, NT, NE])
        mx = sb("mx", [P, NT])
        top = sb("top", [P, NT, NE])
        idx = sb("idx", [P, NT, NE], U32)
        idxf = sb("idxf", [P, NT, 2])
        lane = sb("lane", [P, NE])
        pick = sb("pick", [P, 2, NT, NE])
        pickb = sb("pickb", [P, NT, NE], BF16)
        upper = sb("upper", [P, P], BF16)
        ones = sb("ones", [P, P], BF16)
        base = sb("base", [P, NT, NE])
        rank = sb("rank", [P, NT, NE])
        tot = sb("tot", [P, NT, NE])
        we = sb("we", [P, NE, NT])
        wT = sb("wT", [NE, T])
        ps = ctx.enter_context(nc.psum_tensor("eps8", [P, 8, 512], F32))
        s_xin = sem("e_xin")
        s_small = sem("e_small")
        s_w = [sem(f"e_weights{i}") for i in range(2)]
        s_const = sem("e_const")
        s_add = sem("e_sum")
        s_var = sem("e_var")
        s_ln = sem("e_ln")
        s_guess = sem("e_guess")
        s_z = sem("e_z")
        s_zTf = sem("e_zT_filled")
        s_zTr = sem("e_zT_read")
        s_logit = sem("e_logit")
        s_max = sem("e_max")
        s_exp = sem("e_exp")
        s_pick = sem("e_pick")
        s_count = sem("e_counts")
        s_we = sem("e_gate")
        s_wTf = sem("e_wT_filled")
        s_wTr = sem("e_wT_read")
        s_b2 = sem("e_b2")
        s_b2r = sem("e_b2_read")
        s_hf = sem("e_h_filled")
        s_g = sem("e_gelu")
        s_yf = sem("e_y_filled")
        s_yr = sem("e_y_read")
        s_d = sem("e_dve")
        s_out = sem("e_out")
        FTE = FE // P
        CH = T // S
        blk = ctx.enter_context(nc.Block())

        @blk.sync
        def _(sp):
            sp.dma_start(xin[:, :, :], a["x"].rearrange("(t p) d -> p t d", p=P)).then_inc(s_xin, 16)
            sp.dma_start(rw[:, :, :], a["rw"].rearrange("(k p) e -> p k e", p=P)).then_inc(s_small, 16)
            sp.dma_start(rb[:, :], a["rb"].to_broadcast([P, NE])).then_inc(s_small, 16)
            sp.dma_start(b2[:, :], a["b2"]).then_inc(s_small, 16)
            sp.dma_start(b1[:, :, :], a["b1"]).then_inc(s_small, 16)

            def load(e, i):
                sp.dma_start(w1[:, i, :, :], e(a["w1"]).rearrange("e (k p) f -> p (e k) f", p=P)).then_inc(s_w[i], 16)
                sp.dma_start(w2[:, i, :, :], e(a["w2"]).rearrange("e (k p) f -> p (e k) f", p=P)).then_inc(s_w[i], 16)

            load(lambda ap: ap[0:1], 0)
            load(lambda ap: ap[1:2], 1)
            with sp.Fori(0, NE // 2 - 1) as pair:
                for i in range(2):
                    sp.wait_ge(s_yf, pair * (2 * 2 * CH) + (i + 1) * 2 * CH)
                    load(lambda ap: ap[bass.ds(pair * 2 + (2 + i), 1)], i)
            sp.wait_ge(s_yr, NE * 2 * CH)
            sp.dma_start(out.rearrange("(t p) d -> p t d", p=P), x[:, :, :]).then_inc(s_out, 16)
            sp.wait_ge(s_out, 16)

        @blk.gpsimd
        def _(pool):
            pool.memset(ones[:, :], 1.0).then_inc(s_const, 1)
            pool.memset(upper[:, :], 1.0).then_inc(s_const, 1)
            pool.memset(base[:, 0, :], 0.0).then_inc(s_const, 1)
            for e in range(NE):
                pool.memset(lane[:, e:e + 1], float(e)).then_inc(s_const, 1)
            pool.wait_ge(s_const, 3 + NE)
            pool.affine_select(out=upper[:, :], in_=upper[:, :], compare_op=ALU.is_gt, fill=0.0, base=0,
                               pattern=[[1, P]], channel_multiplier=-1).then_inc(s_const, 1)

        @blk.tensor
        def _(pe):
            for n in range(NT // TT * KD):
                tt, k = divmod(n, KD)
                pe.wait_ge(s_z, TT * tt + TT)
                if n >= 2:
                    pe.wait_ge(s_zTr, n - 1)
                for i in range(TT):
                    tr = nc.tensor.transpose(ps[:, n % 2, i * P:(i + 1) * P], z[:, TT * tt + i, k * P:(k + 1) * P], ident[:, :])
                tr.then_inc(s_zTf, 1)
            pe.wait_ge(s_zTr, NT // TT * KD)
            pe.wait_ge(s_small, 64)
            for t in range(NT):
                for k in range(KD):
                    mm = nc.tensor.matmul(ps[:, 2, t * NE:(t + 1) * NE], zT[:, k, t * P:(t + 1) * P], rw[:, k, :],
                                          start=(k == 0), stop=(k == KD - 1))
            mm.then_inc(s_logit, 1)
            pe.wait_ge(s_pick, 1)
            pe.wait_ge(s_const, 4 + NE)
            picks = pickb[:, :, :].rearrange("p t e -> p (t e)")
            nc.tensor.matmul(ps[:, 3, 0:NT * NE], upper[:, :], picks, start=True, stop=True)
            nc.tensor.matmul(ps[:, 4, 0:NT * NE], ones[:, :], picks, start=True, stop=True).then_inc(s_count, 1)
            pe.wait_ge(s_we, 1)
            for t in range(NT):
                tr = nc.tensor.transpose(ps[0:NE, 4 + t // 4, (t % 4) * P:(t % 4 + 1) * P], we[:, :, t], ident[:, :])
            tr.then_inc(s_wTf, 1)
            pe.wait_ge(s_wTr, 4)
            for n in range(NT // 2):
                if n >= 4:
                    pe.wait_ge(s_b2r, n - 3)
                for i in range(2):
                    t = 2 * n + i
                    mm = nc.tensor.matmul(ps[:, 4 + n % 4, i * D:(i + 1) * D], wT[:, t * P:(t + 1) * P], b2[:, :], start=True, stop=True)
                mm.then_inc(s_b2, 1)
            pe.wait_ge(s_b2r, NT // 2)

            def pair(e0, first):
                for i in range(2):
                    for c in range(CH):
                        n = i * CH + c
                        chunk = e0 * CH + n
                        if c == 0:
                            pe.wait_ge(s_w[i], e0 * 16 + 32)
                        for f in range(FTE):
                            if not (first and n == 0):
                                pe.wait_ge(s_g, chunk * FTE + (f + 1 - FTE))
                            for k in range(KD):
                                mm = nc.tensor.matmul(ps[:, f, :], w1[:, i, k, f * P:(f + 1) * P], zT[:, k, c * S:(c + 1) * S],
                                                      start=(k == 0), stop=(k == KD - 1))
                            mm.then_inc(s_hf, 1)
                        for m in range(2):
                            if not (first and n < 2):
                                pe.wait_ge(s_yr, chunk * 2 + (m - 3))
                            for q in range(2):
                                for f in range(FTE):
                                    if m == 0 and q == 0:
                                        pe.wait_ge(s_g, chunk * FTE + (f + 1))
                                    t = 2 * m + q
                                    mm = nc.tensor.matmul(ps[:, 4 + 2 * (n % 2) + m, q * D:(q + 1) * D], hg[:, n % 2, f, t * P:(t + 1) * P],
                                                          w2[:, i, f, :], start=(f == 0), stop=(f == FTE - 1))
                            mm.then_inc(s_yf, 1)

            pair(0, True)
            with pe.Fori(1, NE // 2) as p:
                pair(p * 2, False)

        @blk.scalar
        def _(act):
            act.preload_act_table_set(EXP_SET)
            act.wait_ge(s_var, 1)
            nc.scalar.activation(lnv[:, :], mv[:, :, 1], ACT.Ln, bias=eps[:, 0:1]).then_inc(s_ln, 1)
            act.wait_ge(s_ln, 1)
            nc.scalar.activation(y0[:, :], lnv[:, :], ACT.Exp, scale=-0.5).then_inc(s_guess, 1)
            for n in range(NT // TT * KD):
                tt, k = divmod(n, KD)
                act.wait_ge(s_zTf, n + 1)
                nc.scalar.activation(zT[:, k, tt * S:(tt + 1) * S], ps[:, n % 2, :], ACT.Copy).then_inc(s_zTr, 1)
            act.wait_ge(s_max, 1)
            nc.scalar.activation(pr[:, :, :], lg[:, :, :], ACT.Exp).then_inc(s_exp, 1)
            act.wait_ge(s_wTf, 1)
            for i in range(4):
                nc.scalar.activation(wT[:, i * S:(i + 1) * S], ps[0:NE, 4 + i, :], ACT.Copy).then_inc(s_wTr, 1)

            def pair(e0, first):
                for i in range(2):
                    for c in range(CH):
                        n = i * CH + c
                        chunk = e0 * CH + n
                        for f in range(FTE):
                            act.wait_ge(s_hf, chunk * FTE + (f + 1))
                            if f == 0 and not (first and n < 2):
                                act.wait_ge(s_yf, chunk * 2 - 2)
                            bias = b1[:, i, f:f + 1] if first else \
                                b1[:, bass.ds(e0 + i, 1), f:f + 1].rearrange("p a b -> p (a b)")
                            nc.scalar.activation(hg[:, n % 2, f, :], ps[:, f, :], ACT.Gelu, bias=bias).then_inc(s_g, 1)

            pair(0, True)
            with act.Fori(1, NE // 2) as p:
                pair(p * 2, False)

        @blk.vector
        def _(dve):
            steps = [0]

            def link(ins):
                steps[0] += 1
                ins.then_inc(s_d, 1)
                dve.wait_ge(s_d, steps[0])

            def each(make, n=NT):
                for t in range(n):
                    ins = make(t)
                    if t < n - 1:
                        steps[0] += 1
                        ins.then_inc(s_d, 1)
                link(ins)

            dve.wait_ge(s_xin, 16)
            link(nc.vector.tensor_tensor(x[:, :, :], x[:, :, :], xin[:, :, :], ALU.add))
            each(lambda t: nc.vector.bn_stats(st[:, t, :], x[:, t, :]))
            each(lambda t: nc.vector.bn_aggr(mv[:, t, :], st[:, t, :]))
            nc.vector.tensor_scalar(ve[:, :], mv[:, :, 1], EPS, None, ALU.add).then_inc(s_var, 1)
            dve.wait_ge(s_guess, 1)
            dve.wait_ge(s_var, 1)
            link(nc.vector.scalar_tensor_tensor(lnv[:, :], y0[:, :], -0.5, y0[:, :], ALU.mult, ALU.mult))
            link(nc.vector.tensor_tensor(lnv[:, :], lnv[:, :], ve[:, :], ALU.mult))
            link(nc.vector.scalar_tensor_tensor(y0[:, :], lnv[:, :], 1.5, y0[:, :], ALU.add, ALU.mult))
            for t in range(NT):
                nc.vector.tensor_scalar(z[:, t, :], x[:, t, :], mv[:, t, 0:1], y0[:, t:t + 1],
                                        ALU.subtract, ALU.mult).then_inc(s_z, 1)
            wide = lambda ap: ap[:, :, None].to_broadcast([P, NT, NE])
            dve.wait_ge(s_small, 64)
            dve.wait_ge(s_logit, 1)
            link(nc.vector.tensor_tensor(lg[:, :, :], ps[:, 2, 0:NT * NE].rearrange("p (t e) -> p t e", e=NE),
                                         rb[:, None, :].to_broadcast([P, NT, NE]), ALU.add))
            link(nc.vector.tensor_reduce(mx[:, :], lg[:, :, :], AX, ALU.max))
            nc.vector.tensor_tensor(lg[:, :, :], lg[:, :, :], wide(mx), ALU.subtract).then_inc(s_max, 1)
            dve.wait_ge(s_exp, 1)
            link(nc.vector.tensor_reduce(mx[:, :], pr[:, :, :], AX, ALU.add))
            link(nc.vector.reciprocal(lnv[:, :], mx[:, :]))
            link(nc.vector.tensor_tensor(pr[:, :, :], pr[:, :, :], wide(lnv), ALU.mult))
            each(lambda t: nc.vector.max(top[:, t, :], pr[:, t, :]))
            each(lambda t: nc.vector.max_index(idx[:, t, :], top[:, t, :], pr[:, t, :]))
            link(nc.vector.tensor_copy(idxf[:, :, :], idx[:, :, 0:2]))
            dve.wait_ge(s_const, 3 + NE)
            for i in range(2):
                link(nc.vector.tensor_tensor(pick[:, i, :, :], lane[:, None, :].to_broadcast([P, NT, NE]),
                                             idxf[:, :, i:i + 1].to_broadcast([P, NT, NE]), ALU.is_equal))
            nc.vector.tensor_tensor(pickb[:, :, :], pick[:, 0, :, :], pick[:, 1, :, :], ALU.add).then_inc(s_pick, 1)
            link(nc.vector.tensor_tensor(mx[:, :], top[:, :, 0], top[:, :, 1], ALU.add))
            link(nc.vector.tensor_scalar(mx[:, :], mx[:, :], 1e-9, None, ALU.max))
            link(nc.vector.reciprocal(lnv[:, :], mx[:, :]))
            link(nc.vector.tensor_tensor(pr[:, :, :], pr[:, :, :], wide(lnv), ALU.mult))
            dve.wait_ge(s_pick, 1)
            link(nc.vector.tensor_tensor(pr[:, :, :], pr[:, :, :], pickb[:, :, :], ALU.mult))
            dve.wait_ge(s_count, 1)
            link(nc.vector.tensor_copy(tot[:, :, :], ps[:, 4, 0:NT * NE].rearrange("p (t e) -> p t e", e=NE)))
            for t in range(1, NT):
                link(nc.vector.tensor_tensor(base[:, t, :], base[:, t - 1, :], tot[:, t - 1, :], ALU.add))
            link(nc.vector.tensor_tensor(rank[:, :, :], base[:, :, :], ps[:, 3, 0:NT * NE].rearrange("p (t e) -> p t e", e=NE), ALU.add))
            nc.vector.scalar_tensor_tensor(we[:, :, :].rearrange("p e t -> p t e"), rank[:, :, :], float(CAP), pr[:, :, :],
                                           ALU.is_lt, ALU.mult).then_inc(s_we, 1)
            for n in range(NT // 2):
                dve.wait_ge(s_b2, n + 1)
                nc.vector.tensor_tensor(x[:, 2 * n:2 * n + 2, :], x[:, 2 * n:2 * n + 2, :],
                                        ps[:, 4 + n % 4, :].rearrange("p (t d) -> p t d", t=2), ALU.add).then_inc(s_b2r, 1)
            dve.wait_ge(s_b2r, NT // 2)
            dve.wait_ge(s_we, 1)

            def pair(e0, first):
                for i in range(2):
                    for c in range(CH):
                        n = i * CH + c
                        chunk = e0 * CH + n
                        for m in range(2):
                            dve.wait_ge(s_yf, chunk * 2 + (m + 1))
                            if not (first and i == 0):
                                dve.wait_ge(s_yr, chunk * 2 + (m + 1 - 2 * CH))
                            for q in range(2):
                                t = TT * c + 2 * m + q
                                gate = we[:, i, t:t + 1] if first else \
                                    we[:, bass.ds(e0 + i, 1), t:t + 1].rearrange("p a b -> p (a b)")
                                ins = nc.vector.scalar_tensor_tensor(x[:, t, :], ps[:, 4 + 2 * (n % 2) + m, q * D:(q + 1) * D], gate,
                                                                     x[:, t, :], ALU.mult, ALU.add)
                            ins.then_inc(s_yr, 1)

            pair(0, True)
            with dve.Fori(1, NE // 2) as p:
                pair(p * 2, False)


def rope_tables():
    half = HD // 2
    inv = np.float32(1.0) / np.power(np.float32(10000.0), (np.arange(half, dtype=np.float32) / np.float32(half))).astype(np.float32)
    ang = (np.arange(S, dtype=np.float32)[:, None] * inv.astype(np.float32)).astype(np.float32)
    rows = np.repeat(ang.T, H, axis=0).astype(np.float64)
    return np.cos(rows).astype(np.float32), np.sin(rows).astype(np.float32)


def kernel(**inputs):
    import concourse.bacc as bacc
    from concourse.bass_utils import run_bass_kernel_spmd

    g = {n: np.asarray(v) for n, v in inputs.items()}
    w = lambda n: g["L0_xcond_" + n]
    c = np.ascontiguousarray
    T_ = lambda m: m.transpose(0, 2, 1)
    order = np.arange(D).reshape(H, 2, HD // 2).transpose(1, 2, 0).reshape(-1)
    qkv = w("qkv_w")
    cos, sin = rope_tables()
    arrays = {
        "x": c(g["x"].reshape(T, D)),
        "condT": c(g["cond_1024"].T),
        "ctxT": c(g["ctx_1024"].reshape(T, D).T),
        "mask": c(g["mask_BxS_bf0"].view(np.uint32)),
        "mask2": c(g["mask_BxS2_bf0"].view(np.uint32)),
        "nwT": c(np.stack([T_(w(f"n{i}_w")) for i in (1, 2, 3)], axis=1).reshape(3 * NL, D, 2 * D)),
        "nb": c(np.stack([w(f"n{i}_b") for i in (1, 2, 3)], axis=1).reshape(3 * NL, 4, P).transpose(2, 0, 1)),
        "wself": c(np.stack([T_(qkv[:, order]), T_(qkv[:, D + order]), T_(qkv[:, 2 * D:]), T_(w("so_w"))], axis=1)),
        "wcross": c(np.stack([T_(w("cq_w")[:, order]), T_(w("ck_w")[:, order]), T_(w("cv_w")), T_(w("co_w"))], axis=1)),
        "f1T": c(T_(w("f1_w"))),
        "f2T": c(T_(w("f2_w"))),
        "f1b": c(w("f1_b").reshape(NL, FT, P).transpose(0, 2, 1)),
        "f2b": c(w("f2_b")),
        "cos": cos,
        "sin": sin,
        "rw": c(g["L0_ffn_router_w"]),
        "rb": c(g["L0_ffn_router_b"].reshape(1, NE)),
        "w1": c(g["L0_ffn_w1"]),
        "b1": c(g["L0_ffn_b1"].reshape(NE, FE // P, P).transpose(2, 0, 1)),
        "w2": c(g["L0_ffn_w2"]),
        "b2": c(g["L0_ffn_b2"]),
    }
    nc = bacc.Bacc("TRN2", target_bir_lowering=False, num_devices=1)
    aps = {n: nc.dram_tensor("in_" + n, v.shape, mybir.dt.from_np(v.dtype), kind="ExternalInput").ap() for n, v in arrays.items()}
    out = nc.dram_tensor("out", (T, D), F32, kind="ExternalOutput").ap()
    nc.disable_value_cache = True
    build(nc, aps, out)
    result = run_bass_kernel_spmd(nc, [{"in_" + n: v for n, v in arrays.items()}], core_ids=[0])
    return result.results[0]["out"].reshape(B, S, D)
```

```python
from contextlib import ExitStack

import numpy as np
import concourse.bass as bass
from concourse import mybir

F32, BF16, U8, U32 = mybir.dt.float32, mybir.dt.bfloat16, mybir.dt.uint8, mybir.dt.uint32
ALU, ACT, AX = mybir.AluOpType, mybir.ActivationFunctionType, mybir.AxisListType.X

NL, D, H, DFF, HD = 6, 256, 16, 1024, 16
B, S = 4, 512
T = B * S
NE, FE, CAP = 8, 512, 640
P = 128
KD = D // P
TT = S // P
NT = T // P
NJ = 2 * B
EPS = 1e-5
RING1 = 3
RING2 = 2
CHUNK_STEPS = (0, 2)
CHUNK_PLACES = {
    "HV": [1, 3], "T1": [4, 5, 6, 7], "HT": [5, 6], "HQ": [7, 8], "HK": [10, 11],
    "T2": [11, 12], "O": [13, 14], "LT": [19, 20],
}
SHIFT_PLACES = (20, 4)
FFN1_PLACES = (22, 28)
FFN2_PLACES = (25, 31)
NORM_STEPS = {
    "HT": dict(stats=[0, 1, 2, 3], aggregate=4, newton=6, tiles=[6, 7, 8, 8]),
    "LT": dict(stats=[30, 31, 32, 33], aggregate=34, newton=35, tiles=[35, 35, 35, 35]),
}
GUESS_PLACES = {"HT": 2, "LT": 18}
SPLIT_PLACES = (10, 12, 16, 18)
PV_STEP = 1
LAST_COPY_STEP = 2

SLOT_UNITS = 16
MASKED = -3.0e38
Q_PARTS = (0, 0, 0, 1, 1, 2)
K_PARTS = (0, 1, 2, 0, 1, 0)
NPROD = len(Q_PARTS)
MASK_ROW = NPROD * HD
SHIFT_ROW = MASK_ROW + 1
ROWS = SHIFT_ROW + 2
VROW = H * (HD + 1) + HD
FT = DFF // P
CHUNKS_PER_LAYER = 192
DVE_PER_LAYER = 196
EXP_SET = "natural_log_exp_and_others"


class Place:

    def __init__(self):
        self.layer = 0

    def at(self, count, per_layer):
        return count + self.layer * per_layer

    def jobs(self, k, per_job):
        return self.at(k * per_job, NJ * per_job)


def is_cross(k):
    return k % NJ >= B


def run_slots(eng, place, head0, slot):
    head0()
    slot(0, p2=False, p1=True, tail=False, head=True)
    slot(1, p2=True, p1=True, tail=False, head=True)
    with eng.Fori(0, NL - 1) as layer:
        place.layer = layer
        for k in range(2, 2 + NJ):
            slot(k, p2=True, p1=True, tail=True, head=True)
    place.layer = NL - 2
    for k in range(2 + NJ, 2 * NJ):
        slot(k, p2=True, p1=True, tail=True, head=k + 1 < 2 * NJ)
    slot(2 * NJ, p2=True, p1=False, tail=True, head=False)
    slot(2 * NJ + 1, p2=False, p1=False, tail=True, head=False)


def build(nc, a, out):
    with ExitStack() as top:
        sb = lambda name, shape, dt=F32: top.enter_context(nc.sbuf_tensor(name, shape, dt))
        x = sb("x", [P, NT, D])
        mod = sb("mod", [P, 3 * NL, 4, B])
        ident = sb("ident", [P, P])
        identb = sb("identb", [P, P], BF16)
        eps = sb("eps", [P, 1])
        maskrow = sb("maskrow", [2 * B, S], BF16)
        prepare(nc, a, x, mod, ident, identb, eps, maskrow)
        layers(nc, a, x, mod, ident, identb, eps, maskrow)
        experts(nc, a, x, ident, eps, out)


def prepare(nc, a, x, mod, ident, identb, eps, maskrow):
    with ExitStack() as ctx:
        sb = lambda name, shape, dt=F32: ctx.enter_context(nc.sbuf_tensor(name, shape, dt))
        sem = lambda name: ctx.enter_context(nc.semaphore(name))
        NN = 3 * NL
        NG = -(-NN // 4)
        condT = sb("condT", [P, KD, 32])
        nw = sb("nw", [P, NN, KD, 2 * D])
        nb = sb("nb", [P, NN, 4])
        gb = sb("gb", [P, NG, 2 * D])
        mask8 = sb("mask8", [2 * B, S // 4], U32)
        st = sb("pst", [P, NT, 6])
        mv = sb("pmv", [P, NT, 2])
        lnv = sb("plnv", [P, NT])
        y0 = sb("py0", [P, NT])
        ve = sb("pve", [P, NT])
        t1 = sb("pt1", [P, NT])
        ps = ctx.enter_context(nc.psum_tensor("pps", [P, 8, 512], F32))
        s_const = sem("p_const")
        s_cond = sem("p_cond")
        s_condz = sem("p_condz")
        s_nw = [sem(f"p_nw{g}") for g in range(NG)]
        s_nb = sem("p_nb")
        s_mask = sem("p_mask")
        s_x = sem("p_x")
        s_gb = sem("p_gb")
        s_gbc = sem("p_gbc")
        s_gbT = sem("p_gbT")
        s_gbfree = sem("p_gbfree")
        s_rs = sem("p_rs")
        s_d = sem("p_dve")
        blk = ctx.enter_context(nc.Block())

        @blk.sync
        def _(sp):
            sp.dma_start(x[:, :, :], a["x"].rearrange("(t p) d -> p t d", p=P)).then_inc(s_x, 16)
            sp.wait_ge(s_condz, 1)
            sp.dma_start(condT[:, :, 0:B], a["condT"].rearrange("(k p) b -> p k b", p=P)).then_inc(s_cond, 16)
            sp.dma_start(mask8[0:B, :], a["mask"]).then_inc(s_mask, 16)
            sp.dma_start(mask8[B:2 * B, :], a["mask2"]).then_inc(s_mask, 16)
            sp.dma_start(nb[:, :, :], a["nb"]).then_inc(s_nb, 16)
            for i in range(NN):
                sp.dma_start(nw[:, i, :, :], a["nwT"][i].rearrange("(k p) o -> p k o", p=P)).then_inc(s_nw[i // 4], 16)

        @blk.gpsimd
        def _(pool):
            pool.memset(condT[:, :, :], 0.0).then_inc(s_condz, 1)
            pool.memset(ident[:, :], 0.0).then_inc(s_const, 1)
            pool.memset(identb[:, :], 0.0).then_inc(s_const, 1)
            pool.memset(eps[:, :], EPS).then_inc(s_const, 1)
            pool.wait_ge(s_const, 3)
            for m in (ident, identb):
                pool.affine_select(out=m[:, :], in_=m[:, :], compare_op=ALU.not_equal, fill=1.0, base=0,
                                   pattern=[[-1, P]], channel_multiplier=1).then_inc(s_const, 1)

        @blk.tensor
        def _(pe):
            pe.wait_ge(s_cond, 16)
            for g in range(NG):
                pe.wait_ge(s_nw[g], 16 * min(4, NN - 4 * g))
                for k in range(KD):
                    for j in range(4):
                        mm = nc.tensor.matmul(ps[32 * j:32 * j + 32, g, :], condT[:, k, :], nw[:, min(4 * g + j, NN - 1), k, :],
                                              start=(k == 0), stop=(k == KD - 1))
                mm.then_inc(s_gb, 1)
            pe.wait_ge(s_const, 5)
            for g in range(NG):
                pe.wait_ge(s_gbc, g + 1)
                if g >= 2:
                    pe.wait_ge(s_gbfree, g - 1)
                for m in range(4):
                    tr = nc.tensor.transpose(ps[:, 5 + g % 2, m * P:(m + 1) * P], gb[:, g, m * P:(m + 1) * P], ident[:, :])
                tr.then_inc(s_gbT, 1)

        @blk.scalar
        def _(act):
            act.preload_act_table_set(EXP_SET)
            for g in range(NG):
                act.wait_ge(s_gb, g + 1)
                nc.scalar.activation(gb[:, g, :], ps[:, g, :], ACT.Copy).then_inc(s_gbc, 1)
            act.wait_ge(s_const, 5)
            act.wait_ge(s_rs, 1)
            nc.scalar.activation(lnv[:, :], mv[:, :, 1], ACT.Ln, bias=eps[:, 0:1]).then_inc(s_rs, 1)
            act.wait_ge(s_rs, 2)
            nc.scalar.activation(y0[:, :], lnv[:, :], ACT.Exp, scale=-0.5).then_inc(s_rs, 1)

        @blk.vector
        def _(dve):
            n = [0]

            def link(ins):
                n[0] += 1
                ins.then_inc(s_d, 1)
                dve.wait_ge(s_d, n[0])

            dve.wait_ge(s_mask, 32)
            nc.vector.tensor_scalar(maskrow[:, :], mask8[:, :].bitcast(U8), MASKED, None, ALU.mult).then_inc(s_d, 1)
            n[0] += 1
            dve.wait_ge(s_x, 16)
            for t in range(NT):
                ins = nc.vector.bn_stats(st[:, t, :], x[:, t, :])
                ins.then_inc(s_d, 1)
            n[0] += NT
            dve.wait_ge(s_d, n[0])
            for t in range(NT):
                nc.vector.bn_aggr(mv[:, t, :], st[:, t, :]).then_inc(s_d, 1)
            n[0] += NT
            dve.wait_ge(s_d, n[0])
            nc.vector.tensor_scalar(ve[:, :], mv[:, :, 1], EPS, None, ALU.add).then_inc(s_rs, 1)
            dve.wait_ge(s_rs, 3)
            link(nc.vector.scalar_tensor_tensor(t1[:, :], y0[:, :], -0.5, y0[:, :], ALU.mult, ALU.mult))
            link(nc.vector.tensor_tensor(t1[:, :], t1[:, :], ve[:, :], ALU.mult))
            link(nc.vector.scalar_tensor_tensor(y0[:, :], t1[:, :], 1.5, y0[:, :], ALU.add, ALU.mult))
            for t in range(NT):
                ins = nc.vector.tensor_scalar(x[:, t, :], x[:, t, :], mv[:, t, 0:1], y0[:, t:t + 1],
                                              ALU.subtract, ALU.mult)
                ins.then_inc(s_d, 1)
            n[0] += NT
            dve.wait_ge(s_nb, 16)
            for g in range(NG):
                dve.wait_ge(s_gbT, g + 1)
                w = min(4, NN - 4 * g)
                for m in range(4):
                    src = ps[:, 5 + g % 2, m * P:m * P + 32 * w].rearrange("p (j c) -> p j c", j=w)[:, :, 0:B]
                    ins = nc.vector.tensor_tensor(mod[:, 4 * g:4 * g + w, m, :], src,
                                                  nb[:, 4 * g:4 * g + w, m:m + 1].to_broadcast([P, w, B]), ALU.add)
                    if m == 3:
                        ins.then_inc(s_gbfree, 1)
                    else:
                        ins.then_inc(s_d, 1)
                        n[0] += 1
            dve.wait_ge(s_gbfree, NG)
            dve.wait_ge(s_d, n[0])
            link(nc.vector.tensor_scalar(mod[:, :, 0:2, :], mod[:, :, 0:2, :], 1.0, None, ALU.add))


def layers(nc, a, x, mod, ident, identb, eps, maskrow):
    with ExitStack() as ctx:
        sb = lambda name, shape, dt=F32: ctx.enter_context(nc.sbuf_tensor(name, shape, dt))
        sem = lambda name: ctx.enter_context(nc.semaphore(name))
        wself = sb("wself", [P, 4, KD, D])
        wcross = sb("wcross", [P, 4, KD, D])
        wf1 = sb("wf1", [P, KD, DFF])
        wf2 = sb("wf2", [P, FT, D])
        f1b = sb("f1b", [P, FT])
        f2b = sb("f2b", [P, D])
        qs = [sb(f"qstack{i}", [ROWS, H, S], BF16) for i in range(2)]
        ks = [sb(f"kstack{i}", [ROWS, H, S], BF16) for i in range(2)]
        parts = sb("parts", [P, 3, KD, S], BF16)
        ropep = sb("ropep", [P, 4, S])
        rot = sb("rot", [P, KD, S])
        prob = sb("prob", [P, 8, S])
        v = [sb(f"v{b}", [P, TT, VROW]) for b in range(B)]
        xnT = sb("xnT", [P, KD, S])
        xnat = sb("xnat", [P, TT, D])
        ctxT = sb("ctxT", [P, KD, S])
        osum = sb("osum", [P, 4, S])
        anat = sb("anat", [P, TT, D])
        hT = sb("hT", [P, FT, S // 2])
        aT = hT[:, 0:4, :].rearrange("p (k a) n -> p k (a n)", k=KD)
        nT = anat[:, :, :].rearrange("p (k a) n -> p k (a n)", k=KD)
        cos = sb("cos", [P, S])
        sin = sb("sin", [P, S])
        negmax = sb("negmax", [P, 2, TT, H // 2])
        mres = sb("mres", [P, 2, TT, H // 2])
        mpart = sb("mpart", [P, 2, TT, 2, H // 2], BF16)
        mrow = sb("mrow", [16, 2, S], BF16)
        recip = sb("recip", [P, TT, H])
        st = sb("st", [P, TT, 6])
        mv = sb("mv", [P, TT, 2])
        lnv = sb("lnv", [P, TT])
        y0 = sb("y0", [P, TT])
        ve = sb("ve", [P, TT])
        fence_at = sb("fence_at", [P, 1])
        bounce = [nc.dram_tensor(f"bounce{i}", (3, D, S), BF16, kind="Internal").ap() for i in range(2)]

        psum = lambda name, n: ctx.enter_context(nc.psum_tensor(name, [P, n, 512], F32))
        ps1 = psum("ps1", RING1)
        ps2 = psum("ps2", RING2)
        psv = psum("psv", 1)
        side = psum("side", 2)

        s_wself = sem("wself_loaded")
        s_wcross = sem("wcross_loaded")
        s_wffn = sem("wffn_loaded")
        s_table = sem("tables_loaded")
        s_ctx = sem("context_loaded")
        s_bounce = [sem(f"bounce_written{i}") for i in range(2)]
        s_stack = [sem(f"stack_loaded{i}") for i in range(2)]
        s_mload = [sem(f"shift_loaded{i}") for i in range(2)]
        s_init = sem("stack_ones_set")
        s_vones = sem("v_ones_set")
        s_p1full = sem("scores_ready")
        s_p1free = sem("scores_reduced")
        s_p2full = sem("shifted_ready")
        s_prob = sem("probs_ready")
        s_pv = sem("pv_unit_done")
        s_os = sem("pv_group_copied")
        s_full = sem("chunk_filled")
        s_read = [sem(f"chunk_read{i}") for i in range(2)]
        s_var = sem("variance_ready")
        s_ln = sem("log_ready")
        s_guess = sem("rstd_guess_ready")
        s_xnat = sem("normed_ready")
        s_rot = sem("rope_done")
        s_hi = sem("high_part_ready")
        s_r1 = sem("high_residual_ready")
        s_mid = sem("mid_part_ready")
        s_low = sem("low_part_ready")
        s_mpart = sem("shift_parts_ready")
        s_bias = sem("ffn_bias_added")
        s_dve = sem("dve_step")
        blk = ctx.enter_context(nc.Block())

        STACK_DMAS = 16 * (2 * NPROD + 1)

        def slot_chunks(k):
            p2, p1 = 1 <= k <= 2 * NJ, k < 2 * NJ
            tail, head = k >= 2, k + 1 < 2 * NJ
            ffn = tail and is_cross(k - 2)
            plan = {i: [] for i in range(2 * SLOT_UNITS)}

            if k == -1:
                plan[0] = [(w, c) for w in ("HT", "HQ", "HK") for c in range(2)]
                return plan
            def put(*names):
                for name in names:
                    for c, at in enumerate(CHUNK_PLACES[name]):
                        plan[at].append((name, c))

            if tail:
                put("T1", "T2", "O")
            if p2:
                plan[SHIFT_PLACES[1]].append(("M", 1))
            if head:
                put("HT", "HQ", "HK")
            if ffn:
                put("LT")
            if p1:
                plan[SHIFT_PLACES[0]].append(("M", 0))
                put("HV")
            if ffn:
                for th in range(2):
                    plan[FFN1_PLACES[th]] += [("F1", c) for c in range(4 * th, 4 * th + 4)]
                    plan[FFN2_PLACES[th]].append(("F2", th))
            return plan

        number, start = {}, {}
        for k in range(-1, 2 * NJ + 2):
            start[k] = len(number)
            for at, names in sorted(slot_chunks(k).items()):
                for name in names:
                    number[(k, *name)] = len(number)
        assert start[2 + NJ] - start[2] == CHUNKS_PER_LAYER

        def wait_filled(eng, place, k, what, c):
            eng.wait_ge(s_full, place.at(number[(k, what, c)] + 1, CHUNKS_PER_LAYER))

        def wait_read(eng, place, k, what, c):
            n = number[(k, what, c)]
            eng.wait_ge(s_read[n % 2], place.at(n // 2 + 1, CHUNKS_PER_LAYER // 2))

        def bank_of(k, what, c):
            n = number[(k, what, c)]
            return side[:, n % 2, :], s_read[n % 2]

        def cross_before(j):
            return (j // NJ) * B + max(0, j % NJ - B) if j > 0 else 0

        def slot_of(j, n, ring):
            return (n + (j % NJ if ring == 3 else 0)) % ring

        def back_of(j, n, ring):
            return (n - 2 if j % NJ or n > 1 else n - 1) if ring == 3 else n - 1

        def norm_index(k, what):
            return min(k + 1, 2 * NJ) + (what == "LT" and k + 1 < 2 * NJ) + cross_before(k - 2)

        def norms(place, k, what, add=0):
            return place.at(norm_index(k, what) + add, NJ + B)

        def norm_row(k, what):
            if what == "LT":
                j = k - 2
                return 3 * (j // NJ) + 2, j % B
            j = k + 1
            return 3 * (j // NJ) + (1 if is_cross(j) else 0), j % B

        @blk.sync
        def _(sp):
            place = Place()

            def at_layer(name, k):
                layer = place.layer + k // NJ
                ap = a[name]
                return ap[bass.ds(layer, 1)] if not isinstance(layer, int) else ap[layer:layer + 1]

            def load_self(k):
                for i in range(4):
                    sp.dma_start(wself[:, i, :, :], at_layer("wself", k)[:, i].rearrange("l (k p) o -> p (l k) o", p=P)).then_inc(s_wself, 16)

            def load_cross_ffn(k):
                for i in range(4):
                    sp.dma_start(wcross[:, i, :, :], at_layer("wcross", k)[:, i].rearrange("l (k p) o -> p (l k) o", p=P)).then_inc(s_wcross, 16)
                sp.dma_start(wf1[:, :, :], at_layer("f1T", k).rearrange("l (k p) o -> p (l k) o", p=P)).then_inc(s_wffn, 16)
                sp.dma_start(wf2[:, :, :], at_layer("f2T", k).rearrange("l (k p) o -> p (l k) o", p=P)).then_inc(s_wffn, 16)
                sp.dma_start(f1b[:, :], at_layer("f1b", k).rearrange("l p f -> p (l f)")).then_inc(s_wffn, 16)
                sp.dma_start(f2b[:, :], at_layer("f2b", k).to_broadcast([P, D])).then_inc(s_wffn, 16)

            def shift_rows(k, j, hf):
                wait_read(sp, place, k, "M", hf)
                for r in range(2):
                    sp.dma_start(qs[j % 2][SHIFT_ROW + r:SHIFT_ROW + r + 1, 8 * hf:8 * hf + 8, :],
                                 mrow[8 * r:8 * r + 8, hf, :]).then_inc(s_mload[hf], 16)

            def write_parts(j):
                for w in range(2):
                    if j > 0 and w == 0:
                        for hf in range(2):
                            sp.wait_ge(s_stack[hf], place.jobs(j, STACK_DMAS))
                    sp.wait_ge(s_low, place.jobs(j, 2) + w + 1)
                    sp.dma_start(bounce[w].rearrange("r (t p) n -> p (r t) n", p=P),
                                 parts[:, :, :, :].rearrange("p r t n -> p (r t) n")).then_inc(s_bounce[w], 16)

            def load_stack(j, hf):
                if hf == 0:
                    for w in range(2):
                        sp.wait_ge(s_bounce[w], place.jobs(j + 1, 16))
                if j >= 2:
                    sp.wait_ge(s_p2full, place.jobs(j - 2, 64) + 32 * (hf + 1))
                heads = slice(8 * hf, 8 * hf + 8)
                for w, (stack, order) in enumerate(((qs, Q_PARTS), (ks, K_PARTS))):
                    for r, part in enumerate(order):
                        sp.dma_start(stack[j % 2][HD * r:HD * (r + 1), heads, :],
                                     bounce[w][part].rearrange("(c h) n -> c h n", h=H)[:, heads, :]).then_inc(s_stack[hf], 16)
                row = j % NJ
                sp.dma_start(ks[j % 2][MASK_ROW:MASK_ROW + 1, heads, :],
                             maskrow[row:row + 1, None, :].to_broadcast([1, 8, S])).then_inc(s_stack[hf], 16)

            def head0():
                load_self(0)
                sp.dma_start(cos[:, :], a["cos"]).then_inc(s_table, 16)
                sp.dma_start(sin[:, :], a["sin"]).then_inc(s_table, 16)
                sp.wait_ge(s_init, 2)
                write_parts(0)
                load_stack(0, 0)
                load_stack(0, 1)

            def slot(k, p2, p1, tail, head):
                side_done = place.at(start[k], CHUNKS_PER_LAYER)
                if k % NJ == 2 and p1:
                    sp.wait_ge(s_full, side_done)
                    load_cross_ffn(k)
                if head and is_cross(k + 1):
                    wait_filled(sp, place, k, "HV", 1)
                    b = (k + 1) % B
                    sp.dma_start(ctxT[:, :, :], a["ctxT"].rearrange("(k p) n -> p k n", p=P)[:, :, b * S:(b + 1) * S]).then_inc(s_ctx, 16)
                if k % NJ == 6 and k < NJ:
                    sp.wait_ge(s_full, side_done)
                    load_self(k + NJ)
                if p2:
                    shift_rows(k, k - 1, 1)
                if k == 0:
                    sp.wait_ge(s_init, 4)
                if head:
                    write_parts(k + 1)
                    load_stack(k + 1, 0)
                if p1:
                    shift_rows(k, k, 0)
                if head:
                    load_stack(k + 1, 1)

            run_slots(sp, place, head0, slot)

        @blk.gpsimd
        def _(pool):
            place = Place()

            def stack_ones(i):
                pool.memset(qs[i][MASK_ROW:ROWS, :, :], 1.0).then_inc(s_init, 1)
                pool.memset(ks[i][MASK_ROW:ROWS, :, :], 1.0).then_inc(s_init, 1)

            stack_ones(0)
            pool.wait_ge(s_init, 2)

            def split(k, j, w):
                done = place.jobs(j, 2) + w
                wait_read(pool, place, k, ("HQ", "HK")[w], 1)
                if j or w:
                    pool.wait_ge(s_mid, done)
                    pool.wait_ge(s_low, done)
                nc.gpsimd.tensor_tensor(rot[:, 0, :], ropep[:, 0, :], ropep[:, 1, :], ALU.subtract).then_inc(s_rot, 1)
                nc.gpsimd.tensor_tensor(rot[:, 1, :], ropep[:, 2, :], ropep[:, 3, :], ALU.add).then_inc(s_rot, 1)
                pool.wait_ge(s_hi, done + 1)
                nc.gpsimd.tensor_tensor(rot[:, :, :], rot[:, :, :], parts[:, 0, :, :], ALU.subtract).then_inc(s_r1, 1)
                pool.wait_ge(s_mid, done + 1)
                nc.gpsimd.tensor_tensor(parts[:, 2, :, :], rot[:, :, :], parts[:, 1, :, :], ALU.subtract).then_inc(s_low, 1)

            def head0():
                split(-1, 0, 0)
                split(-1, 0, 1)
                pool.wait_ge(s_low, 2)
                stack_ones(1)
                pool.wait_ge(s_init, 4)

            def slot(k, p2, p1, tail, head):
                if head:
                    split(k, k + 1, 0)
                    split(k, k + 1, 1)
                if tail and is_cross(k - 2):
                    j = k - 2
                    tiles = slice(TT * (j % B), TT * (j % B + 1))
                    pool.wait_ge(s_xnat, norms(place, k, "LT", 1))
                    pool.wait_ge(s_wffn, place.at(64 * (j // NJ + 1), 64))
                    nc.gpsimd.tensor_tensor(x[:, tiles, :], x[:, tiles, :], f2b[:, None, :].to_broadcast([P, TT, D]),
                                            ALU.add).then_inc(s_bias, 1)

            run_slots(pool, place, head0, slot)

        @blk.tensor
        def _(pe):
            place = Place()

            def begin(k, what, c):
                n = number[(k, what, c)]
                if n >= 2:
                    pe.wait_ge(s_read[n % 2], place.at(n // 2, CHUNKS_PER_LAYER // 2))
                return side[:, n % 2, :]

            def transposes(bank, tiles):
                for i, tile in enumerate(tiles):
                    tr = nc.tensor.transpose(bank[:, i * P:(i + 1) * P], tile, ident[:, :])
                tr.then_inc(s_full, 1)

            def project_T(bank, w, act_T, m):
                for k in range(KD):
                    mm = nc.tensor.matmul(bank, w[:, k, m * P:(m + 1) * P], act_T[:, k, :], start=(k == 0), stop=(k == KD - 1))
                mm.then_inc(s_full, 1)

            def project(bank, w, act_T, t0, nk):
                for i in range(2):
                    t = t0 + i
                    for k in range(nk):
                        mm = nc.tensor.matmul(bank[:, i * D:(i + 1) * D], act_T[:, k, t * P:(t + 1) * P], w[:, k, :],
                                              start=(k == 0), stop=(k == nk - 1))
                mm.then_inc(s_full, 1)

            def side_work(k, what, c):
                if what == "T1":
                    if c == 0:
                        pe.wait_ge(s_os, place.jobs(k - 1, 4))
                    transposes(begin(k, what, c), [osum[:, g, c * P:(c + 1) * P] for g in range(4)])
                elif what == "T2":
                    if c == 0:
                        wait_read(pe, place, k, "T1", 2)
                        wait_read(pe, place, k, "T1", 3)
                    transposes(begin(k, what, c), [anat[:, t, c * P:(c + 1) * P] for t in range(TT)])
                elif what == "O":
                    if c == 0:
                        wait_read(pe, place, k, "T2", 0)
                        wait_read(pe, place, k, "T2", 1)
                    w = wcross if is_cross(k - 2) else wself
                    project(begin(k, what, c), w[:, 3], aT, 2 * c, KD)
                elif what in ("HT", "LT"):
                    if c == 0:
                        pe.wait_ge(s_xnat, norms(place, k, what, 1))
                    transposes(begin(k, what, c), [xnat[:, t, c * P:(c + 1) * P] for t in range(TT)])
                elif what in ("HQ", "HK", "HV"):
                    j = k if what == "HV" else k + 1
                    i = ("HQ", "HK", "HV").index(what)
                    if i == 0 and c == 0:
                        wait_read(pe, place, k, "HT", 0)
                        wait_read(pe, place, k, "HT", 1)
                        pe.wait_ge(s_wcross if is_cross(j) else s_wself, place.at(64 * (j // NJ + 1), 64))
                    if i == 1 and c == 0 and is_cross(j):
                        pe.wait_ge(s_ctx, place.at(16 * (cross_before(j) + 1), 16 * B))
                    src = ctxT if is_cross(j) and i > 0 else xnT
                    w = (wcross if is_cross(j) else wself)[:, i]
                    if i < 2:
                        project_T(begin(k, what, c), w, src, c)
                    else:
                        project(begin(k, what, c), w, src, 2 * c, KD)
                elif what == "M":
                    j = k - 1 if c == 1 else k
                    pe.wait_ge(s_mpart, place.jobs(j, 2) + c + 1)
                    bank = begin(k, what, c)
                    for t in range(TT):
                        mm = nc.tensor.matmul(bank[0:16, t * P:(t + 1) * P], mpart[:, c, t, :, :].rearrange("p a b -> p (a b)"),
                                              identb[:, :], start=True, stop=True)
                    mm.then_inc(s_full, 1)
                elif what == "F1":
                    th, cc = divmod(c, 4)
                    if c == 0:
                        wait_read(pe, place, k, "LT", 0)
                        wait_read(pe, place, k, "LT", 1)
                        pe.wait_ge(s_wffn, place.at(64 * ((k - 2) // NJ + 1), 64))
                    bank = begin(k, what, c)
                    for i in range(2):
                        f = 2 * cc + i
                        for kk in range(KD):
                            mm = nc.tensor.matmul(bank[:, i * D:(i + 1) * D], wf1[:, kk, f * P:(f + 1) * P],
                                                  nT[:, kk, th * (S // 2):(th + 1) * (S // 2)],
                                                  start=(kk == 0), stop=(kk == KD - 1))
                    mm.then_inc(s_full, 1)
                elif what == "F2":
                    wait_read(pe, place, k, "F1", 4 * c + 2)
                    wait_read(pe, place, k, "F1", 4 * c + 3)
                    project(begin(k, what, c), wf2, hT, 0, FT)

            def pass2(j, u, i):
                g, kt = divmod(u, TT)
                q, kk = qs[j % 2], ks[j % 2]
                if u % 8 == 0 and i == 0:
                    pe.wait_ge(s_mload[u // 8], place.jobs(j + 1, 32))
                h, n = 4 * g + i, 4 * u + i
                back = back_of(j, n, RING2)
                if j > 0 or n >= RING2:
                    pe.wait_ge(s_prob, place.jobs(j, 64) + back)
                nc.tensor.matmul(ps2[:, slot_of(j, n, RING2), :], kk[:, h, kt * P:(kt + 1) * P], q[:, h, :],
                                 start=True, stop=True).then_inc(s_p2full, 1)

            def pv(j, u):
                g, kt = divmod(u, TT)
                if kt == 0 and (j > 0 or u > 0):
                    pe.wait_ge(s_os, place.jobs(j, 4) + g)
                pe.wait_ge(s_prob, place.jobs(j, 64) + 4 * u + 4)
                for i in range(4):
                    h = 4 * g + i
                    mm = nc.tensor.matmul(psv[32 * i:32 * i + 32, 0, :], v[j % B][:, kt, (HD + 1) * h:(HD + 1) * h + 32],
                                          prob[:, 4 * (u % 2) + i, :], start=(kt == 0), stop=(kt == TT - 1))
                mm.then_inc(s_pv, 1)

            def pass1(j, h, t):
                if h % 8 == 0 and t == 0:
                    pe.wait_ge(s_stack[h // 8], place.jobs(j + 1, STACK_DMAS))
                q, kk = qs[j % 2], ks[j % 2]
                n = TT * h + t
                if j > 0 or n >= RING1:
                    pe.wait_ge(s_p1free, place.jobs(j, 64) + back_of(j, n, RING1))
                nc.tensor.matmul(ps1[:, slot_of(j, n, RING1), :], q[0:SHIFT_ROW, h, t * P:(t + 1) * P], kk[0:SHIFT_ROW, h, :],
                                 start=True, stop=True).then_inc(s_p1full, 1)

            def head0():
                for what, c in slot_chunks(-1)[0]:
                    side_work(-1, what, c)
                pe.wait_ge(s_vones, B)

            def slot(k, p2, p1, tail, head):
                plan = slot_chunks(k)
                for u in range(SLOT_UNITS):
                    for i in range(TT):
                        if p1:
                            pass1(k, u, i)
                        if p2:
                            pass2(k - 1, u, i)
                        if i == PV_STEP:
                            if u and p2:
                                pv(k - 1, u - 1)
                            elif u == 0 and tail:
                                pv(k - 2, SLOT_UNITS - 1)
                        if i in CHUNK_STEPS:
                            for what, c in plan[2 * u + CHUNK_STEPS.index(i)]:
                                side_work(k, what, c)

            run_slots(pe, place, head0, slot)

        @blk.scalar
        def _(act):
            place = Place()
            act.preload_act_table_set(EXP_SET)

            def exp(j, u, i):
                n = 4 * u + i
                act.wait_ge(s_p2full, place.jobs(j, 64) + n + 1)
                if i == 0 and (j > 0 or u >= 2):
                    act.wait_ge(s_pv, place.jobs(j, 16) + u - 1)
                nc.scalar.activation(prob[:, 4 * (u % 2) + i, :], ps2[:, slot_of(j, n, RING2), :], ACT.Exp,
                                     scale=HD ** -0.5).then_inc(s_prob, 1)

            def copy_group(k, j, g):
                if g == 0 and k >= 2:
                    wait_filled(act, place, k, "T1", 3)
                act.wait_ge(s_pv, place.jobs(j, 16) + 4 * g + 4)
                nc.scalar.activation(osum[:, g, :], psv[:, 0, :], ACT.Copy).then_inc(s_os, 1)

            def rstd_guess(k, what):
                act.wait_ge(s_var, norms(place, k, what, 1))
                nc.scalar.activation(lnv[:, :], mv[:, :, 1], ACT.Ln, bias=eps[:, 0:1]).then_inc(s_ln, 1)
                act.wait_ge(s_ln, norms(place, k, what, 1))
                nc.scalar.activation(y0[:, :], lnv[:, :], ACT.Exp, scale=-0.5).then_inc(s_guess, 1)

            def modulate(k, what, c):
                wait_filled(act, place, k, what, c)
                bank, read = bank_of(k, what, c)
                row, b = norm_row(k, what)
                layer = place.layer
                if isinstance(layer, int):
                    g = mod[:, row + 3 * layer, c, b:b + 1]
                    be = mod[:, row + 3 * layer, KD + c, b:b + 1]
                else:
                    i = layer * 3 + row
                    g = mod[:, bass.ds(i, 1), c, b:b + 1].rearrange("p a b -> p (a b)")
                    be = mod[:, bass.ds(i, 1), KD + c, b:b + 1].rearrange("p a b -> p (a b)")
                nc.scalar.activation((nT if what == "LT" else xnT)[:, c, :], bank, ACT.Identity, scale=g, bias=be).then_inc(read, 1)

            def hi(j, w):
                done = place.jobs(j, 2) + w
                act.wait_ge(s_rot, place.jobs(j, 4) + 2 * w + 2)
                if w == 1:
                    act.wait_ge(s_bounce[0], place.jobs(j + 1, 16))
                elif j > 0:
                    act.wait_ge(s_bounce[1], place.jobs(j, 16))
                nc.scalar.activation(parts[:, 0, :, :], rot[:, :, :], ACT.Copy).then_inc(s_hi, 1)

            def mid(j, w):
                act.wait_ge(s_r1, place.jobs(j, 2) + w + 1)
                nc.scalar.activation(parts[:, 1, :, :], rot[:, :, :], ACT.Copy).then_inc(s_mid, 1)

            def side_work(k, what, c):
                if what in ("HT", "LT"):
                    modulate(k, what, c)
                elif what == "T2":
                    wait_filled(act, place, k, what, c)
                    bank, read = bank_of(k, what, c)
                    nc.scalar.activation(aT[:, c, :], bank, ACT.Copy).then_inc(read, 1)
                elif what == "HV":
                    wait_filled(act, place, k, what, c)
                    bank, read = bank_of(k, what, c)
                    j = k
                    dst = v[j % B][:, 2 * c:2 * c + 2, 0:H * (HD + 1)].rearrange("p t (h e) -> p t h e", h=H)[:, :, :, 0:HD]
                    nc.scalar.activation(dst, bank.rearrange("p (t h d) -> p t h d", t=2, h=H), ACT.Copy).then_inc(read, 1)
                elif what == "M":
                    j = k - 1 if c == 1 else k
                    wait_filled(act, place, k, what, c)
                    bank, read = bank_of(k, what, c)
                    if j > 0:
                        act.wait_ge(s_mload[c], place.jobs(j, 32))
                    nc.scalar.activation(mrow[:, c, :], bank[0:16, :], ACT.Copy).then_inc(read, 1)
                elif what == "F1":
                    wait_filled(act, place, k, what, c)
                    bank, read = bank_of(k, what, c)
                    for i in range(2):
                        f = 2 * (c % 4) + i
                        ins = nc.scalar.activation(hT[:, f, :], bank[:, i * D:(i + 1) * D], ACT.Gelu, bias=f1b[:, f:f + 1])
                    ins.then_inc(read, 1)
                    if c % 4 == 3:
                        act.preload_act_table_set(EXP_SET)

            def head0():
                rstd_guess(-1, "HT")
                for c in range(2):
                    modulate(-1, "HT", c)
                hi(0, 0)
                mid(0, 0)
                hi(0, 1)
                mid(0, 1)

            def slot(k, p2, p1, tail, head):
                plan = slot_chunks(k)
                ffn = tail and is_cross(k - 2)
                for u in range(SLOT_UNITS):
                    for i in range(4):
                        if p2:
                            exp(k - 1, u, i)
                            if i == PV_STEP and u and u % TT == 0:
                                copy_group(k, k - 1, u // TT - 1)
                        if tail and 4 * u + i == LAST_COPY_STEP:
                            copy_group(k, k - 2, TT - 1)
                        if i not in CHUNK_STEPS:
                            continue
                        at = 2 * u + CHUNK_STEPS.index(i)
                        for what, c in plan[at]:
                            side_work(k, what, c)
                        if head and at == GUESS_PLACES["HT"]:
                            rstd_guess(k, "HT")
                        if ffn and at == GUESS_PLACES["LT"]:
                            rstd_guess(k, "LT")
                        if head and at == SPLIT_PLACES[0]:
                            hi(k + 1, 0)
                        if head and at == SPLIT_PLACES[1]:
                            mid(k + 1, 0)
                        if head and at == SPLIT_PLACES[2]:
                            hi(k + 1, 1)
                        if head and at == SPLIT_PLACES[3]:
                            mid(k + 1, 1)

            run_slots(act, place, head0, slot)

        @blk.vector
        def _(dve):
            place = Place()
            steps = [0]

            def step(ins):
                steps[0] += 1
                ins.then_inc(s_dve, 1)
                return steps[0]

            def wait_step(n):
                dve.wait_ge(s_dve, place.at(n, DVE_PER_LAYER))

            def stats(k, what, t):
                j = k - 2 if what == "LT" else k + 1
                if t == 0:
                    if what == "LT":
                        wait_read(dve, place, k, "O", 1)
                    elif steps[0]:
                        wait_step(steps[0])
                step(nc.vector.bn_stats(st[:, t, :], x[:, TT * (j % B) + t, :]))

            def aggregate(what):
                wait_step(steps[0])
                nc.vector.memset(fence_at[:, :], 0.0)
                for t in range(TT):
                    n = step(nc.vector.bn_aggr(mv[:, t, :], st[:, t, :]))
                wait_step(n)
                nc.vector.tensor_scalar(ve[:, :], mv[:, :, 1], EPS, None, ALU.add).then_inc(s_var, 1)

            def normalise(k, what):
                j = k - 2 if what == "LT" else k + 1
                dve.wait_ge(s_guess, norms(place, k, what, 1))
                wait_step(step(nc.vector.scalar_tensor_tensor(lnv[:, :], y0[:, :], -0.5, y0[:, :], ALU.mult, ALU.mult)))
                wait_step(step(nc.vector.tensor_tensor(lnv[:, :], lnv[:, :], ve[:, :], ALU.mult)))
                wait_step(step(nc.vector.scalar_tensor_tensor(y0[:, :], lnv[:, :], 1.5, y0[:, :], ALU.add, ALU.mult)))

            def normed(k, what, t):
                j = k - 2 if what == "LT" else k + 1
                ins = nc.vector.tensor_scalar(xnat[:, t, :], x[:, TT * (j % B) + t, :], mv[:, t, 0:1], y0[:, t:t + 1],
                                              ALU.subtract, ALU.mult)
                if t == TT - 1:
                    ins.then_inc(s_xnat, 1)

            def maximum(j, h, t):
                n = TT * h + t
                dve.wait_ge(s_p1full, place.jobs(j, 64) + n + 1)
                nc.vector.tensor_reduce(negmax[:, h // 8, t, h % 8:h % 8 + 1], ps1[:, slot_of(j, n, RING1), :], AX, ALU.max,
                                        negate=True).then_inc(s_p1free, 1)

            def shift_parts(j, hf):
                dve.wait_ge(s_p1free, place.jobs(j, 64) + 32 * (hf + 1))
                wait_step(step(nc.vector.tensor_copy(mpart[:, hf, :, 0, :], negmax[:, hf, :, :])))
                wait_step(step(nc.vector.tensor_tensor(mres[:, hf, :, :], negmax[:, hf, :, :], mpart[:, hf, :, 0, :], ALU.subtract)))
                nc.vector.tensor_copy(mpart[:, hf, :, 1, :], mres[:, hf, :, :]).then_inc(s_mpart, 1)

            def side_work(k, what, c):
                if what not in ("T1", "HQ", "HK", "O", "F2"):
                    return
                wait_filled(dve, place, k, what, c)
                bank, read = bank_of(k, what, c)
                if what == "T1":
                    heads = bank.rearrange("p (h e) -> p h e", h=H)
                    wait_step(step(nc.vector.reciprocal(recip[:, c, :], heads[:, :, HD])))
                    nc.vector.tensor_tensor(anat[:, c, :].rearrange("p (h d) -> p h d", h=H), heads[:, :, 0:HD],
                                            recip[:, c, :, None].to_broadcast([P, H, HD]), ALU.mult).then_inc(read, 1)
                elif what in ("HQ", "HK"):
                    j, w = k + 1, int(what == "HK")
                    if c == 0:
                        if j == 0 and w == 0:
                            dve.wait_ge(s_table, 32)
                        else:
                            dve.wait_ge(s_rot, place.jobs(j, 4) + 2 * w)
                    first, second = (cos, sin) if c == 0 else (sin, cos)
                    nc.vector.tensor_tensor(ropep[:, c, :], bank, first[:, :], ALU.mult)
                    nc.vector.tensor_tensor(ropep[:, 2 + c, :], bank, second[:, :], ALU.mult).then_inc(read, 1)
                else:
                    j = k - 2
                    t0 = TT * (j % B) + 2 * c
                    if what == "F2" and c == 0:
                        dve.wait_ge(s_bias, place.at(cross_before(j) + 1, B))
                    nc.vector.tensor_tensor(x[:, t0:t0 + 2, :], x[:, t0:t0 + 2, :], bank.rearrange("p (t d) -> p t d", t=2),
                                            ALU.add).then_inc(read, 1)

            def head0():
                for t in range(TT):
                    stats(-1, "HT", t)
                aggregate("HT")
                normalise(-1, "HT")
                for t in range(TT):
                    normed(-1, "HT", t)
                for what, c in slot_chunks(-1)[0]:
                    side_work(-1, what, c)
                for b in range(B):
                    nc.vector.memset(v[b][:, :, :], 1.0).then_inc(s_vones, 1)

            def slot(k, p2, p1, tail, head):
                if k == 2:
                    steps_at_loop[0] = steps[0]
                if k == 2 + NJ:
                    assert steps[0] - steps_at_loop[0] == DVE_PER_LAYER, steps[0] - steps_at_loop[0]
                plan = slot_chunks(k)
                ffn = tail and is_cross(k - 2)
                for u in range(SLOT_UNITS):
                    for i in range(TT):
                        if p1:
                            maximum(k, u, i)
                            if u == 8 and i == 1:
                                shift_parts(k, 0)
                        at = 4 * u + i
                        for what, wanted in (("HT", head), ("LT", ffn)):
                            steps_of = NORM_STEPS[what]
                            if not wanted:
                                continue
                            if at in steps_of["stats"]:
                                stats(k, what, steps_of["stats"].index(at))
                            if at == steps_of["aggregate"]:
                                aggregate(what)
                            if at == steps_of["newton"]:
                                normalise(k, what)
                            for t in range(TT):
                                if at == steps_of["tiles"][t]:
                                    normed(k, what, t)
                        if i not in CHUNK_STEPS:
                            continue
                        at = 2 * u + CHUNK_STEPS.index(i)
                        for what, c in plan[at]:
                            side_work(k, what, c)
                if p1:
                    shift_parts(k, 1)

            steps_at_loop = [0]
            run_slots(dve, place, head0, slot)




def experts(nc, a, x, ident, eps, out):
    with ExitStack() as ctx:
        sb = lambda name, shape, dt=F32: ctx.enter_context(nc.sbuf_tensor(name, shape, dt))
        sem = lambda name: ctx.enter_context(nc.semaphore(name))
        xin = sb("xin", [P, NT, D])
        z = sb("z", [P, NT, D])
        zT = sb("zT", [P, KD, T])
        rw = sb("rw", [P, KD, NE])
        rb = sb("rb", [P, NE])
        b2 = sb("b2", [NE, D])
        b1 = sb("b1", [P, NE, FE // P])
        w1 = sb("w1", [P, 2, KD, FE])
        w2 = sb("w2", [P, 2, FE // P, D])
        hg = sb("hg", [P, 2, FE // P, S])
        st = sb("est", [P, NT, 6])
        mv = sb("emv", [P, NT, 2])
        lnv = sb("elnv", [P, NT])
        y0 = sb("ey0", [P, NT])
        ve = sb("eve", [P, NT])
        lg = sb("lg", [P, NT, NE])
        pr = sb("pr", [P, NT, NE])
        mx = sb("mx", [P, NT])
        top = sb("top", [P, NT, NE])
        idx = sb("idx", [P, NT, NE], U32)
        idxf = sb("idxf", [P, NT, 2])
        lane = sb("lane", [P, NE])
        pick = sb("pick", [P, 2, NT, NE])
        pickb = sb("pickb", [P, NT, NE], BF16)
        upper = sb("upper", [P, P], BF16)
        ones = sb("ones", [P, P], BF16)
        base = sb("base", [P, NT, NE])
        rank = sb("rank", [P, NT, NE])
        tot = sb("tot", [P, NT, NE])
        we = sb("we", [P, NE, NT])
        wT = sb("wT", [NE, T])
        ps = ctx.enter_context(nc.psum_tensor("eps8", [P, 8, 512], F32))
        s_xin = [sem(f"e_xin{i}") for i in range(NT // TT)]
        s_small = sem("e_small")
        s_w = [sem(f"e_weights{i}") for i in range(2)]
        s_const = sem("e_const")
        s_add = sem("e_sum")
        s_var = sem("e_var")
        s_ln = sem("e_ln")
        s_guess = sem("e_guess")
        s_z = sem("e_z")
        s_zTf = sem("e_zT_filled")
        s_zTr = sem("e_zT_read")
        s_logit = sem("e_logit")
        s_max = sem("e_max")
        s_exp = sem("e_exp")
        s_pick = sem("e_pick")
        s_count = sem("e_counts")
        s_we = sem("e_gate")
        s_wTf = sem("e_wT_filled")
        s_wTr = sem("e_wT_read")
        s_b2 = sem("e_b2")
        s_b2r = sem("e_b2_read")
        s_hf = sem("e_h_filled")
        s_g = sem("e_gelu")
        s_yf = sem("e_y_filled")
        s_yr = sem("e_y_read")
        s_d = sem("e_dve")
        s_out = sem("e_out")
        FTE = FE // P
        CH = T // S
        blk = ctx.enter_context(nc.Block())

        @blk.sync
        def _(sp):
            x_tiles = a["x"].rearrange("(t p) d -> p t d", p=P)
            for i in range(NT // TT):
                tiles = slice(TT * i, TT * (i + 1))
                sp.dma_start(xin[:, tiles, :], x_tiles[:, tiles, :]).then_inc(s_xin[i], 16)
            sp.dma_start(rw[:, :, :], a["rw"].rearrange("(k p) e -> p k e", p=P)).then_inc(s_small, 16)
            sp.dma_start(rb[:, :], a["rb"].to_broadcast([P, NE])).then_inc(s_small, 16)
            sp.dma_start(b2[:, :], a["b2"]).then_inc(s_small, 16)
            sp.dma_start(b1[:, :, :], a["b1"]).then_inc(s_small, 16)

            def load(e, i):
                sp.dma_start(w1[:, i, :, :], e(a["w1"]).rearrange("e (k p) f -> p (e k) f", p=P)).then_inc(s_w[i], 16)
                sp.dma_start(w2[:, i, :, :], e(a["w2"]).rearrange("e (k p) f -> p (e k) f", p=P)).then_inc(s_w[i], 16)

            load(lambda ap: ap[0:1], 0)
            load(lambda ap: ap[1:2], 1)
            with sp.Fori(0, NE // 2 - 1) as pair:
                for i in range(2):
                    sp.wait_ge(s_yf, pair * (2 * 2 * CH) + (i + 1) * 2 * CH)
                    load(lambda ap: ap[bass.ds(pair * 2 + (2 + i), 1)], i)
            out_tiles = out.rearrange("(t p) d -> p t d", p=P)
            for n in range(2 * CH):
                sp.wait_ge(s_yr, (NE - 1) * 2 * CH + n + 1)
                sp.dma_start(out_tiles[:, 2 * n:2 * n + 2, :], x[:, 2 * n:2 * n + 2, :]).then_inc(s_out, 16)
            sp.wait_ge(s_out, 16 * 2 * CH)

        @blk.gpsimd
        def _(pool):
            pool.memset(ones[:, :], 1.0).then_inc(s_const, 1)
            pool.memset(upper[:, :], 1.0).then_inc(s_const, 1)
            pool.memset(base[:, 0, :], 0.0).then_inc(s_const, 1)
            for e in range(NE):
                pool.memset(lane[:, e:e + 1], float(e)).then_inc(s_const, 1)
            pool.wait_ge(s_const, 3 + NE)
            pool.affine_select(out=upper[:, :], in_=upper[:, :], compare_op=ALU.is_gt, fill=0.0, base=0,
                               pattern=[[1, P]], channel_multiplier=-1).then_inc(s_const, 1)

        @blk.tensor
        def _(pe):
            for n in range(NT // TT * KD):
                tt, k = divmod(n, KD)
                pe.wait_ge(s_z, TT * tt + TT)
                if n >= 2:
                    pe.wait_ge(s_zTr, n - 1)
                for i in range(TT):
                    tr = nc.tensor.transpose(ps[:, n % 2, i * P:(i + 1) * P], z[:, TT * tt + i, k * P:(k + 1) * P], ident[:, :])
                tr.then_inc(s_zTf, 1)
            pe.wait_ge(s_zTr, NT // TT * KD)
            pe.wait_ge(s_small, 64)
            for t in range(NT):
                for k in range(KD):
                    mm = nc.tensor.matmul(ps[:, 2, t * NE:(t + 1) * NE], zT[:, k, t * P:(t + 1) * P], rw[:, k, :],
                                          start=(k == 0), stop=(k == KD - 1))
            mm.then_inc(s_logit, 1)
            pe.wait_ge(s_pick, 1)
            pe.wait_ge(s_const, 4 + NE)
            picks = pickb[:, :, :].rearrange("p t e -> p (t e)")
            nc.tensor.matmul(ps[:, 3, 0:NT * NE], upper[:, :], picks, start=True, stop=True)
            nc.tensor.matmul(ps[:, 4, 0:NT * NE], ones[:, :], picks, start=True, stop=True).then_inc(s_count, 1)
            pe.wait_ge(s_we, 1)
            for t in range(NT):
                tr = nc.tensor.transpose(ps[0:NE, 4 + t // 4, (t % 4) * P:(t % 4 + 1) * P], we[:, :, t], ident[:, :])
            tr.then_inc(s_wTf, 1)
            pe.wait_ge(s_wTr, 4)
            for n in range(NT // 2):
                if n >= 4:
                    pe.wait_ge(s_b2r, n - 3)
                for i in range(2):
                    t = 2 * n + i
                    mm = nc.tensor.matmul(ps[:, 4 + n % 4, i * D:(i + 1) * D], wT[:, t * P:(t + 1) * P], b2[:, :], start=True, stop=True)
                mm.then_inc(s_b2, 1)
            pe.wait_ge(s_b2r, NT // 2)

            def pair(e0, first):
                for i in range(2):
                    for c in range(CH):
                        n = i * CH + c
                        chunk = e0 * CH + n
                        if c == 0:
                            pe.wait_ge(s_w[i], e0 * 16 + 32)
                        for f in range(FTE):
                            if not (first and n == 0):
                                pe.wait_ge(s_g, chunk * FTE + (f + 1 - FTE))
                            for k in range(KD):
                                mm = nc.tensor.matmul(ps[:, f, :], w1[:, i, k, f * P:(f + 1) * P], zT[:, k, c * S:(c + 1) * S],
                                                      start=(k == 0), stop=(k == KD - 1))
                            mm.then_inc(s_hf, 1)
                        for m in range(2):
                            if not (first and n < 2):
                                pe.wait_ge(s_yr, chunk * 2 + (m - 3))
                            for q in range(2):
                                for f in range(FTE):
                                    if m == 0 and q == 0:
                                        pe.wait_ge(s_g, chunk * FTE + (f + 1))
                                    t = 2 * m + q
                                    mm = nc.tensor.matmul(ps[:, 4 + 2 * (n % 2) + m, q * D:(q + 1) * D], hg[:, n % 2, f, t * P:(t + 1) * P],
                                                          w2[:, i, f, :], start=(f == 0), stop=(f == FTE - 1))
                            mm.then_inc(s_yf, 1)

            pair(0, True)
            with pe.Fori(1, NE // 2) as p:
                pair(p * 2, False)

        @blk.scalar
        def _(act):
            act.preload_act_table_set(EXP_SET)
            act.wait_ge(s_var, 1)
            nc.scalar.activation(lnv[:, :], mv[:, :, 1], ACT.Ln, bias=eps[:, 0:1]).then_inc(s_ln, 1)
            act.wait_ge(s_ln, 1)
            nc.scalar.activation(y0[:, :], lnv[:, :], ACT.Exp, scale=-0.5).then_inc(s_guess, 1)
            for n in range(NT // TT * KD):
                tt, k = divmod(n, KD)
                act.wait_ge(s_zTf, n + 1)
                nc.scalar.activation(zT[:, k, tt * S:(tt + 1) * S], ps[:, n % 2, :], ACT.Copy).then_inc(s_zTr, 1)
            act.wait_ge(s_max, 1)
            nc.scalar.activation(pr[:, :, :], lg[:, :, :], ACT.Exp).then_inc(s_exp, 1)
            act.wait_ge(s_wTf, 1)
            for i in range(4):
                nc.scalar.activation(wT[:, i * S:(i + 1) * S], ps[0:NE, 4 + i, :], ACT.Copy).then_inc(s_wTr, 1)

            def pair(e0, first):
                for i in range(2):
                    for c in range(CH):
                        n = i * CH + c
                        chunk = e0 * CH + n
                        for f in range(FTE):
                            act.wait_ge(s_hf, chunk * FTE + (f + 1))
                            if f == 0 and not (first and n < 2):
                                act.wait_ge(s_yf, chunk * 2 - 2)
                            bias = b1[:, i, f:f + 1] if first else \
                                b1[:, bass.ds(e0 + i, 1), f:f + 1].rearrange("p a b -> p (a b)")
                            nc.scalar.activation(hg[:, n % 2, f, :], ps[:, f, :], ACT.Gelu, bias=bias).then_inc(s_g, 1)

            pair(0, True)
            with act.Fori(1, NE // 2) as p:
                pair(p * 2, False)

        @blk.vector
        def _(dve):
            steps = [0]

            def link(ins):
                steps[0] += 1
                ins.then_inc(s_d, 1)
                dve.wait_ge(s_d, steps[0])

            def each(make, n=NT):
                for t in range(n):
                    ins = make(t)
                    if t < n - 1:
                        steps[0] += 1
                        ins.then_inc(s_d, 1)
                link(ins)

            for i in range(NT // TT):
                tiles = slice(TT * i, TT * (i + 1))
                dve.wait_ge(s_xin[i], 16)
                link(nc.vector.tensor_tensor(x[:, tiles, :], x[:, tiles, :], xin[:, tiles, :], ALU.add))
            each(lambda t: nc.vector.bn_stats(st[:, t, :], x[:, t, :]))
            each(lambda t: nc.vector.bn_aggr(mv[:, t, :], st[:, t, :]))
            nc.vector.tensor_scalar(ve[:, :], mv[:, :, 1], EPS, None, ALU.add).then_inc(s_var, 1)
            dve.wait_ge(s_guess, 1)
            dve.wait_ge(s_var, 1)
            link(nc.vector.scalar_tensor_tensor(lnv[:, :], y0[:, :], -0.5, y0[:, :], ALU.mult, ALU.mult))
            link(nc.vector.tensor_tensor(lnv[:, :], lnv[:, :], ve[:, :], ALU.mult))
            link(nc.vector.scalar_tensor_tensor(y0[:, :], lnv[:, :], 1.5, y0[:, :], ALU.add, ALU.mult))
            for t in range(NT):
                nc.vector.tensor_scalar(z[:, t, :], x[:, t, :], mv[:, t, 0:1], y0[:, t:t + 1],
                                        ALU.subtract, ALU.mult).then_inc(s_z, 1)
            wide = lambda ap: ap[:, :, None].to_broadcast([P, NT, NE])
            dve.wait_ge(s_small, 64)
            dve.wait_ge(s_logit, 1)
            link(nc.vector.tensor_tensor(lg[:, :, :], ps[:, 2, 0:NT * NE].rearrange("p (t e) -> p t e", e=NE),
                                         rb[:, None, :].to_broadcast([P, NT, NE]), ALU.add))
            link(nc.vector.tensor_reduce(mx[:, :], lg[:, :, :], AX, ALU.max))
            nc.vector.tensor_tensor(lg[:, :, :], lg[:, :, :], wide(mx), ALU.subtract).then_inc(s_max, 1)
            dve.wait_ge(s_exp, 1)
            link(nc.vector.tensor_reduce(mx[:, :], pr[:, :, :], AX, ALU.add))
            link(nc.vector.reciprocal(lnv[:, :], mx[:, :]))
            link(nc.vector.tensor_tensor(pr[:, :, :], pr[:, :, :], wide(lnv), ALU.mult))
            each(lambda t: nc.vector.max(top[:, t, :], pr[:, t, :]))
            each(lambda t: nc.vector.max_index(idx[:, t, :], top[:, t, :], pr[:, t, :]))
            link(nc.vector.tensor_copy(idxf[:, :, :], idx[:, :, 0:2]))
            dve.wait_ge(s_const, 3 + NE)
            for i in range(2):
                link(nc.vector.tensor_tensor(pick[:, i, :, :], lane[:, None, :].to_broadcast([P, NT, NE]),
                                             idxf[:, :, i:i + 1].to_broadcast([P, NT, NE]), ALU.is_equal))
            nc.vector.tensor_tensor(pickb[:, :, :], pick[:, 0, :, :], pick[:, 1, :, :], ALU.add).then_inc(s_pick, 1)
            link(nc.vector.tensor_tensor(mx[:, :], top[:, :, 0], top[:, :, 1], ALU.add))
            link(nc.vector.tensor_scalar(mx[:, :], mx[:, :], 1e-9, None, ALU.max))
            link(nc.vector.reciprocal(lnv[:, :], mx[:, :]))
            link(nc.vector.tensor_tensor(pr[:, :, :], pr[:, :, :], wide(lnv), ALU.mult))
            dve.wait_ge(s_pick, 1)
            link(nc.vector.tensor_tensor(pr[:, :, :], pr[:, :, :], pickb[:, :, :], ALU.mult))
            dve.wait_ge(s_count, 1)
            link(nc.vector.tensor_copy(tot[:, :, :], ps[:, 4, 0:NT * NE].rearrange("p (t e) -> p t e", e=NE)))
            for t in range(1, NT):
                link(nc.vector.tensor_tensor(base[:, t, :], base[:, t - 1, :], tot[:, t - 1, :], ALU.add))
            link(nc.vector.tensor_tensor(rank[:, :, :], base[:, :, :], ps[:, 3, 0:NT * NE].rearrange("p (t e) -> p t e", e=NE), ALU.add))
            nc.vector.scalar_tensor_tensor(we[:, :, :].rearrange("p e t -> p t e"), rank[:, :, :], float(CAP), pr[:, :, :],
                                           ALU.is_lt, ALU.mult).then_inc(s_we, 1)
            for n in range(NT // 2):
                dve.wait_ge(s_b2, n + 1)
                nc.vector.tensor_tensor(x[:, 2 * n:2 * n + 2, :], x[:, 2 * n:2 * n + 2, :],
                                        ps[:, 4 + n % 4, :].rearrange("p (t d) -> p t d", t=2), ALU.add).then_inc(s_b2r, 1)
            dve.wait_ge(s_b2r, NT // 2)
            dve.wait_ge(s_we, 1)

            def pair(e0, first):
                for i in range(2):
                    for c in range(CH):
                        n = i * CH + c
                        chunk = e0 * CH + n
                        for m in range(2):
                            dve.wait_ge(s_yf, chunk * 2 + (m + 1))
                            if not (first and i == 0):
                                dve.wait_ge(s_yr, chunk * 2 + (m + 1 - 2 * CH))
                            for q in range(2):
                                t = TT * c + 2 * m + q
                                gate = we[:, i, t:t + 1] if first else \
                                    we[:, bass.ds(e0 + i, 1), t:t + 1].rearrange("p a b -> p (a b)")
                                ins = nc.vector.scalar_tensor_tensor(x[:, t, :], ps[:, 4 + 2 * (n % 2) + m, q * D:(q + 1) * D], gate,
                                                                     x[:, t, :], ALU.mult, ALU.add)
                            ins.then_inc(s_yr, 1)

            pair(0, True)
            with dve.Fori(1, NE // 2) as p:
                pair(p * 2, False)


def rope_tables():
    half = HD // 2
    inv = np.float32(1.0) / np.power(np.float32(10000.0), (np.arange(half, dtype=np.float32) / np.float32(half))).astype(np.float32)
    ang = (np.arange(S, dtype=np.float32)[:, None] * inv.astype(np.float32)).astype(np.float32)
    rows = np.repeat(ang.T, H, axis=0).astype(np.float64)
    return np.cos(rows).astype(np.float32), np.sin(rows).astype(np.float32)


def kernel(**inputs):
    import concourse.bacc as bacc
    from concourse.bass_utils import run_bass_kernel_spmd

    g = {n: np.asarray(v) for n, v in inputs.items()}
    w = lambda n: g["L0_xcond_" + n]
    c = np.ascontiguousarray
    T_ = lambda m: m.transpose(0, 2, 1)
    order = np.arange(D).reshape(H, 2, HD // 2).transpose(1, 2, 0).reshape(-1)
    qkv = w("qkv_w")
    cos, sin = rope_tables()
    arrays = {
        "x": c(g["x"].reshape(T, D)),
        "condT": c(g["cond_1024"].T),
        "ctxT": c(g["ctx_1024"].reshape(T, D).T),
        "mask": c(g["mask_BxS_bf0"].view(np.uint32)),
        "mask2": c(g["mask_BxS2_bf0"].view(np.uint32)),
        "nwT": c(np.stack([T_(w(f"n{i}_w")) for i in (1, 2, 3)], axis=1).reshape(3 * NL, D, 2 * D)),
        "nb": c(np.stack([w(f"n{i}_b") for i in (1, 2, 3)], axis=1).reshape(3 * NL, 4, P).transpose(2, 0, 1)),
        "wself": c(np.stack([T_(qkv[:, order]), T_(qkv[:, D + order]), T_(qkv[:, 2 * D:]), T_(w("so_w"))], axis=1)),
        "wcross": c(np.stack([T_(w("cq_w")[:, order]), T_(w("ck_w")[:, order]), T_(w("cv_w")), T_(w("co_w"))], axis=1)),
        "f1T": c(T_(w("f1_w"))),
        "f2T": c(T_(w("f2_w"))),
        "f1b": c(w("f1_b").reshape(NL, FT, P).transpose(0, 2, 1)),
        "f2b": c(w("f2_b")),
        "cos": cos,
        "sin": sin,
        "rw": c(g["L0_ffn_router_w"]),
        "rb": c(g["L0_ffn_router_b"].reshape(1, NE)),
        "w1": c(g["L0_ffn_w1"]),
        "b1": c(g["L0_ffn_b1"].reshape(NE, FE // P, P).transpose(2, 0, 1)),
        "w2": c(g["L0_ffn_w2"]),
        "b2": c(g["L0_ffn_b2"]),
    }
    nc = bacc.Bacc("TRN2", target_bir_lowering=False, num_devices=1)
    aps = {n: nc.dram_tensor("in_" + n, v.shape, mybir.dt.from_np(v.dtype), kind="ExternalInput").ap() for n, v in arrays.items()}
    out = nc.dram_tensor("out", (T, D), F32, kind="ExternalOutput").ap()
    nc.disable_value_cache = True
    build(nc, aps, out)
    result = run_bass_kernel_spmd(nc, [{"in_" + n: v for n, v in arrays.items()}], core_ids=[0])
    return result.results[0]["out"].reshape(B, S, D)
```
